# Optimizing a Trainium2 kernel written in Bass

```python
import numpy as np
import jax
import jax.numpy as jnp

def _softmax(x, axis=-1):
    return jax.nn.softmax(x, axis=axis)

def _gelu(x):
    return jax.nn.gelu(x, approximate=True)

def _silu(x):
    return jax.nn.silu(x)

def _sigmoid(x):
    return jax.nn.sigmoid(x)

def _layernorm(x, axis=-1, eps=1e-05):
    m = jnp.mean(x, axis=axis, keepdims=True)
    v = jnp.var(x, axis=axis, keepdims=True)
    return (x - m) / jnp.sqrt(v + eps)

def _scatter_add(tgt, idx, src, axis=0):
    return tgt.at[idx].add(src)

def _segment_sum(src, seg, n):
    return jax.ops.segment_sum(src, seg, n)
kernel_name = 'mk_seq_preln_d1_jaxref_r4_6c3fa7'

def setup_inputs(seed: int=0):
    np.random.seed(seed)
    _w = jnp.asarray

    def _L0_attn_setup():
        import jax, jax.numpy as jnp
        import numpy as np
        WIDTH = 256
        NUM_HEADS = 16
        HEAD_DIM = WIDTH // NUM_HEADS
        WINDOW = 64
        BATCH = 2
        SEQ = 512
        _MIN_LOGITS_VALUE = -1e+30
        key = jax.random.key(seed)
        ks = jax.random.split(key, 6)
        std = 1.0 / np.sqrt(WIDTH)
        x = jax.random.normal(ks[0], (BATCH, SEQ, WIDTH), dtype=jnp.float32)
        Wq = jax.random.normal(ks[1], (WIDTH, WIDTH), dtype=jnp.float32) * std
        Wk = jax.random.normal(ks[2], (HEAD_DIM, WIDTH), dtype=jnp.float32) * std
        Wv = jax.random.normal(ks[3], (HEAD_DIM, WIDTH), dtype=jnp.float32) * std
        Wf = jax.random.normal(ks[4], (WIDTH, WIDTH), dtype=jnp.float32) * std
        bf = jnp.zeros((WIDTH,), dtype=jnp.float32)
        return {'x': x, 'Wq': Wq, 'Wk': Wk, 'Wv': Wv, 'Wf': Wf, 'bf': bf}
    _L0_attn_in = _L0_attn_setup()

    def _L0_ffn_setup():
        import jax, jax.numpy as jnp
        import numpy as np
        ALPHA = 1.0
        key = jax.random.key(seed)
        ks = jax.random.split(key, 7)
        B, S, IN, OUT = (8, 2048, 256, 256)
        RANK, DDIM, UDIM = (4, 100, 50)
        return {'hidden_states': jax.random.normal(ks[0], (B, S, IN), dtype=jnp.float32), 'W': jax.random.normal(ks[1], (OUT, IN), dtype=jnp.float32) * 0.02, 'b': jax.random.normal(ks[2], (OUT,), dtype=jnp.float32) * 0.02, 'lora_down': jax.random.normal(ks[3], (RANK, DDIM), dtype=jnp.float32) * 0.1, 'lora_up': jax.random.normal(ks[4], (UDIM, RANK), dtype=jnp.float32) * 0.1, 'down_aux': jax.random.normal(ks[5], (DDIM, IN), dtype=jnp.float32) * 0.03, 'up_aux': jax.random.normal(ks[6], (OUT, UDIM), dtype=jnp.float32) * 0.03}
    _L0_ffn_in = _L0_ffn_setup()
    _d = {'L0_attn_x': _L0_attn_in['x'], 'L0_attn_Wq': _L0_attn_in['Wq'], 'L0_attn_Wk': _L0_attn_in['Wk'], 'L0_attn_Wv': _L0_attn_in['Wv'], 'L0_attn_Wf': _L0_attn_in['Wf'], 'L0_attn_bf': _L0_attn_in['bf'], 'L0_ffn_W': _L0_ffn_in['W'], 'L0_ffn_b': _L0_ffn_in['b'], 'L0_ffn_lora_down': _L0_ffn_in['lora_down'], 'L0_ffn_lora_up': _L0_ffn_in['lora_up'], 'L0_ffn_down_aux': _L0_ffn_in['down_aux'], 'L0_ffn_up_aux': _L0_ffn_in['up_aux']}
    _x0 = _d['L0_attn_x']
    _d['L0_attn_x'] = jax.random.normal(jax.random.fold_in(jax.random.key(seed), 1), (4, 2048, 256), dtype=_x0.dtype)
    del _x0
    return _d

def reference(L0_attn_x, L0_attn_Wq, L0_attn_Wk, L0_attn_Wv, L0_attn_Wf, L0_attn_bf, L0_ffn_W, L0_ffn_b, L0_ffn_lora_down, L0_ffn_lora_up, L0_ffn_down_aux, L0_ffn_up_aux):

    def _L0_attn_ref(x, Wq, Wk, Wv, Wf, bf):
        import jax, jax.numpy as jnp
        import numpy as np
        WIDTH = 256
        NUM_HEADS = 16
        HEAD_DIM = WIDTH // NUM_HEADS
        WINDOW = 64
        BATCH = 2
        SEQ = 512
        _MIN_LOGITS_VALUE = -1e+30
        b, t, _ = x.shape
        q = (x @ Wq.T).reshape(b, t, NUM_HEADS, HEAD_DIM)
        k = x @ Wk.T
        v = x @ Wv.T
        scale = 1.0 / np.sqrt(HEAD_DIM)
        logits = jnp.einsum('btnh,bsh->bnts', q, k) * scale
        pos = jnp.arange(t)
        mask = jnp.abs(pos[:, None] - pos[None, :]) <= WINDOW
        masked = jnp.where(mask[None, None, :, :], logits, _MIN_LOGITS_VALUE)
        probs = jax.nn.softmax(masked.astype(jnp.float32), axis=-1).astype(logits.dtype)
        out = jnp.einsum('bnts,bsh->btnh', probs, v).reshape(b, t, WIDTH)
        return out @ Wf.T + bf

    def _L0_ffn_ref(hidden_states, W, b, lora_down, lora_up, down_aux, up_aux):
        import jax, jax.numpy as jnp
        import numpy as np
        ALPHA = 1.0
        lilora_weight = up_aux @ (lora_up @ (lora_down @ down_aux))
        base = jnp.einsum('bsi,oi->bso', hidden_states, W) + b
        delta = jnp.einsum('bsi,oi->bso', hidden_states, lilora_weight)
        return base + ALPHA * delta
    x = L0_attn_x
    x = x + _L0_attn_ref(_layernorm(x, axis=-1), L0_attn_Wq, L0_attn_Wk, L0_attn_Wv, L0_attn_Wf, L0_attn_bf)
    x = x + _L0_ffn_ref(_layernorm(x, axis=-1), L0_ffn_W, L0_ffn_b, L0_ffn_lora_down, L0_ffn_lora_up, L0_ffn_down_aux, L0_ffn_up_aux)
    return x

_drawn_inputs = setup_inputs


def setup_inputs(seed=0):
    import zlib

    import numpy as np

    out = dict(_drawn_inputs(seed))
    spreads = {'L0_attn_bf': (0.0, 0.1)}
    factors = {'L0_ffn_b': 2.966,
     'L0_ffn_lora_down': 3.012,
     'L0_ffn_lora_up': 3.366,
     'L0_ffn_down_aux': 3.17,
     'L0_ffn_up_aux': 3.12}
    for name, (base, spread) in spreads.items():
        noise = np.random.default_rng([zlib.crc32(name.encode()), seed]).standard_normal(out[name].shape)
        drawn = base * np.exp(spread * noise) if base else spread * noise
        out[name] = jnp.asarray(drawn.astype(out[name].dtype))
    for name, factor in factors.items():
        out[name] = (out[name] * factor).astype(out[name].dtype)
    return out
```

```python
from contextlib import ExitStack

import concourse.bass as bass
from concourse import mybir

F32 = mybir.dt.float32
BF16 = mybir.dt.bfloat16
ALU = mybir.AluOpType
ACT = mybir.ActivationFunctionType
AX = mybir.AxisListType

P = 128
BATCH, SEQ, WIDTH = 4, 2048, 256
HEADS, HD = 16, 16
WINDOW = 64
TOKENS = BATCH * SEQ
TILE = 512
TILES = TOKENS // TILE
TJ = TILE // P
BLOCKS = TOKENS // P
BPS = SEQ // P
GQ = 32
GROUPS = P // GQ
GWIN = GQ + 2 * WINDOW
KWIN = P + 2 * WINDOW
LP = SEQ + 2 * WINDOW
VW = 32
PARTS = 3
KROWS = 6 * HD
KEDGE = KROWS + 1
KALL = KEDGE + PARTS
FC = WIDTH // P
RING = 4
UNITS = 2 * GROUPS
STU = GROUPS + 1
NEG = -1.0e30
EPS = 1e-5
SCALE = HD ** -0.5
DDIM, UDIM, RANK = 100, 50, 4

Q_DMAS = 6
K_DMAS = 4
M_DMAS = PARTS


def wait(engine, semaphore, value):
    if isinstance(value, int) and value <= 0:
        return
    engine.wait_ge(semaphore, value)


def there(i, n):
    return not isinstance(i, int) or 0 <= i < n


def seen(count):
    return min(count, BLOCKS) if isinstance(count, int) else count


def build(nc, x, wq_t, wkv_t, wf_t, bf_rows, wffn_t, b_rows, down_t, up_t, down_aux, up_aux_t,
          edge_rows, onehot, corners, rem_mask, onehot_cols, ident, ident_b, out):
    q_scr = nc.dram_tensor("q_scratch", (PARTS, WIDTH, TOKENS), BF16, kind="Internal").ap()
    k_scr = nc.dram_tensor("k_scratch", (PARTS, HD, BATCH * LP), BF16, kind="Internal").ap()
    v_scr = nc.dram_tensor("v_scratch", (BATCH * LP, VW), F32, kind="Internal").ap()

    ctx = ExitStack()
    with ctx:
        def sb(name, shape, dt=F32):
            return ctx.enter_context(nc.sbuf_tensor(name, shape, dt))

        def sem(name):
            return ctx.enter_context(nc.semaphore(name))

        wq = sb("wq", [P, FC, WIDTH])
        wkv = sb("wkv", [P, FC, P])
        wf = sb("wf", [P, FC, WIDTH])
        bf_bc = sb("bf_bc", [P, WIDTH])
        b_bc = sb("b_bc", [P, WIDTH])
        wffn = sb("wffn", [P, FC, WIDTH])
        weff = sb("weff", [P, FC, WIDTH])
        downT = sb("downT", [DDIM, RANK])
        upT = sb("upT", [RANK, UDIM])
        daux = sb("daux", [DDIM, WIDTH])
        uauxT = sb("uauxT", [UDIM, WIDTH])
        low1 = sb("low1", [RANK, WIDTH])
        low2 = sb("low2", [UDIM, WIDTH])
        hot = sb("hot", [GQ, P], BF16)
        corner = sb("corner", [GQ, 2, 2, GQ], BF16)
        remm = sb("remm", [GQ, P], BF16)
        hotc = sb("hotc", [GQ, HEADS * GQ], BF16)
        idf = sb("idf", [P, P])
        idb = sb("idb", [P, P], BF16)
        tick = sb("tick", [1, 1])
        neghalf = sb("neghalf", [P, TJ])
        bdmask = sb("bdmask", [P, GROUPS, VW])
        zero = sb("zero", [P, P])

        xt = sb("xt", [P, 2, TJ, WIDTH])
        st1 = sb("st1", [P, TJ, 6])
        mv1 = sb("mv1", [P, TJ, 2])
        ve1 = sb("ve1", [P, TJ])
        rs1 = sb("rs1", [P, TJ])
        xn = sb("xn", [P, 2, TJ, WIDTH])
        xnT = sb("xnT", [P, 2, FC, TILE])
        qp = sb("qp", [P, 2, PARTS, FC, TILE], BF16)
        qr = sb("qr", [P, FC, TILE])
        kvS = sb("kvS", [P, TILE])
        kp = sb("kp", [HD, 2, PARTS, TILE], BF16)
        kr = sb("kr", [HD, TILE])
        vn = sb("vn", [P, 2, TJ, VW])

        qin = sb("qin", [KROWS, 2, HEADS, 2 * P], BF16)
        qs = sb("qs", [KALL, RING, GROUPS, HEADS, GQ], BF16)
        ks = sb("ks", [KALL, RING, KWIN], BF16)
        vm = sb("vm", [P, RING, GROUPS, VW])
        vx = sb("vx", [P, RING, VW])
        vbd = sb("vbd", [P, 2, GROUPS, VW])
        xr = sb("xr", [P, RING, WIDTH])
        mx = sb("mx", [P, 2, 16])
        mp = sb("mp", [P, P // 16, 16], BF16)
        mr = sb("mr", [P, 2, 16])
        mt = sb("mt", [PARTS * 16, 2, P], BF16)
        pm = sb("pm", [P, 2, GROUPS, HEADS * GQ])
        pr = sb("pr", [P, 2, HEADS * GQ])
        ot = sb("ot", [P, TILE])
        rden = sb("rden", [P, 4, 4])
        on = sb("on", [P, WIDTH])
        onT = sb("onT", [P, FC, P])
        x2 = sb("x2", [P, WIDTH])
        st2 = sb("st2", [P, 6])
        mv2 = sb("mv2", [P, 2])
        ve2 = sb("ve2", [P, 1])
        rs2 = sb("rs2", [P, 1])
        x2n = sb("x2n", [P, WIDTH])
        x2nT = sb("x2nT", [P, FC, P])
        x2b = sb("x2b", [P, WIDTH])
        ob = sb("ob", [P, 2, WIDTH])

        bank = [ctx.enter_context(nc.psum_tensor(f"bank{i}", [P, 512], F32)) for i in range(5)]
        qbank = ctx.enter_context(nc.psum_tensor("qbank", [P, FC, 512], F32))
        b7 = ctx.enter_context(nc.psum_tensor("bank7", [P, 512], F32))
        sbank, tbank, pvbank, otbank, trbank, dbank = bank[0:2], bank[2:4], bank[4], qbank[:, 0], qbank[:, 1], b7

        s_const = sem("s_const")
        s_set = sem("s_set")
        s_zero = sem("s_zero")
        s_halo = sem("s_halo")
        s_low = sem("s_low")
        s_lowc = sem("s_lowc")
        s_weff = sem("s_weff")

        s_x1 = [sem(f"s_x1_{i}") for i in range(2)]
        s_st1, s_mv1, s_ve1, s_rs1, s_xn = (sem(n) for n in ("s_st1", "s_mv1", "s_ve1", "s_rs1", "s_xn"))
        s_tr1, s_xnT, s_q, s_kv, s_vt = (sem(n) for n in ("s_tr1", "s_xnT", "s_q", "s_kv", "s_vt"))
        s_q1, s_qr, s_q2, s_q3 = (sem(n) for n in ("s_q1", "s_qr", "s_q2", "s_q3"))
        s_kvs, s_k1, s_kr, s_k2, s_k3, s_vn = (sem(n) for n in ("s_kvs", "s_k1", "s_kr", "s_k2", "s_k3", "s_vn"))
        s_stq = [sem(f"s_stq{i}") for i in range(2)]

        s_qin = [sem(f"s_qin{i}") for i in range(2)]
        s_qs = sem("s_qs")
        s_k = [sem(f"s_k_{i}") for i in range(RING)]
        s_v = [sem(f"s_v{i}") for i in range(RING)]
        s_xin = [sem(f"s_xin{i}") for i in range(RING)]
        s_m = [sem(f"s_m{i}") for i in range(RING)]
        s_out = [sem(f"s_out{i}") for i in range(2)]
        s_sc, s_mx, s_mp1, s_mr1, s_mp2, s_mr2, s_mp = (sem(n) for n in (
            "s_sc", "s_mx", "s_mp1", "s_mr1", "s_mp2", "s_mr2", "s_mp"))
        s_mtp, s_mt = sem("s_mtp"), sem("s_mt")
        s_stp, s_ex, s_sel, s_vbd = (sem(n) for n in ("s_stp", "s_ex", "s_sel", "s_vbd"))
        s_pv, s_ot, s_otp, s_rd, s_on = (sem(n) for n in ("s_pv", "s_ot", "s_otp", "s_rd", "s_on"))
        s_ntp, s_onT, s_wf, s_xb, s_x2, s_st2, s_mv2, s_ve2, s_rs2 = (sem(n) for n in (
            "s_ntp", "s_onT", "s_wf", "s_xb", "s_x2", "s_st2", "s_mv2", "s_ve2", "s_rs2"))
        s_x2n, s_xtp, s_x2nT, s_ffn, s_x2b, s_ob = (sem(n) for n in (
            "s_x2n", "s_xtp", "s_x2nT", "s_ffn", "s_x2b", "s_ob"))

        consts = [
            (wq[:], wq_t.rearrange("(c p) n -> p c n", p=P)), (wkv[:], wkv_t.rearrange("(c p) n -> p c n", p=P)),
            (wf[:], wf_t.rearrange("(c p) n -> p c n", p=P)), (wffn[:], wffn_t.rearrange("(c p) n -> p c n", p=P)),
            (bf_bc[:], bf_rows), (b_bc[:], b_rows), (downT[:], down_t), (upT[:], up_t), (daux[:], down_aux),
            (uauxT[:], up_aux_t), (hot[:], onehot), (corner[:], corners), (remm[:], rem_mask),
            (hotc[:], onehot_cols), (idf[:], ident), (idb[:], ident_b),
        ]
        CONST = 16 * len(consts)

        block = ctx.enter_context(nc.Block())

        def p1_loop(engine, step):
            for s in range(-2, 4):
                step(s, s % 2)
            with engine.Fori(2, TILES // 2 - 1) as i:
                for u in range(2):
                    step(2 * i + u, u)
            for s in range(TILES - 2, TILES + 1):
                step(s, s % 2)

        def p2_loop(engine, step):
            for n in range(-1, 8):
                step(n, n % 4)
            with engine.Fori(2, BLOCKS // 4 - 1) as t:
                for u in range(4):
                    step(4 * t + u, u)
            for n in range(BLOCKS - 4, BLOCKS + 5):
                step(n, n % 4)

        @block.sync
        def _(sp):
            for dst, src in consts:
                sp.dma_start(dst, src).then_inc(s_const, 16)
            sp.wait_ge(s_zero, 1)
            n_halo = 0
            for b in range(BATCH):
                for at in (b * LP, b * LP + WINDOW + SEQ):
                    sp.dma_start(k_scr[:, :, at:at + WINDOW].rearrange("a d w -> (a d) w"),
                                 zero[0:PARTS * HD, 0:WINDOW // 2].bitcast(BF16)).then_inc(s_halo, 16)
                    sp.dma_start(v_scr[at:at + WINDOW, :], zero[0:WINDOW, 0:VW]).then_inc(s_halo, 16)
                    n_halo += 32

            def p1(s, par):
                ld, pj, vt = s + 2, s, s - 1
                if there(ld, TILES):
                    wait(sp, s_xn, ld - 1)
                    sp.dma_start(xt[:, par], x[bass.ds(ld * TILE, TILE), :].rearrange("(j p) f -> p j f", p=P)
                                 ).then_inc(s_x1[par], 16)
                if there(pj, TILES):
                    wait(sp, s_q3, pj + 1)
                    for a in range(PARTS):
                        sp.dma_start(q_scr[a, :, bass.ds(pj * TILE, TILE)].rearrange("(c p) t -> p c t", p=P),
                                     qp[:, par, a]).then_inc(s_stq[par], 16)
                    wait(sp, s_k3, pj + 1)
                    at = pj * TILE + (pj // 4) * (LP - SEQ) + WINDOW
                    sp.dma_start(k_scr[:, :, bass.ds(at, TILE)].rearrange("a d t -> d a t"),
                                 kp[:, par]).then_inc(s_stq[par], 16)
                if there(vt, TILES):
                    wait(sp, s_vn, vt + 1)
                    at = vt * TILE + (vt // 4) * (LP - SEQ) + WINDOW
                    sp.dma_start(v_scr[bass.ds(at, TILE), :].rearrange("(j p) c -> p j c", p=P),
                                 vn[:, 1 - par]).then_inc(s_stq[1 - par], 16)

            p1_loop(sp, p1)

            sp.wait_ge(s_halo, n_halo)
            for par in range(2):
                sp.wait_ge(s_stq[par], 5 * 16 * TILES // 2)
            sp.wait_ge(s_set, 2)

            def p2(n, u):
                a, vb, xb_, m, e = n, n - 1, n - 2, n - 2, n - 5
                if u % 2 == 0 and there(a, BLOCKS):
                    wait(sp, s_qs, a - 2)
                    row = 0
                    for part, copies in ((0, 3), (1, 2), (2, 1)):
                        for _ in range(copies):
                            sp.dma_start(qin[row:row + HD, u // 2],
                                         q_scr[part, :, bass.ds(a * P, 2 * P)].rearrange("(h d) t -> d h t", d=HD)
                                         ).then_inc(s_qin[u // 2], 16)
                            row += HD
                if there(a, BLOCKS):
                    wait(sp, s_stp, STU * (a - 3))
                    sl = u
                    at = a * P + (a // BPS) * (LP - SEQ)
                    row = 0
                    for parts in (3, 2, 1):
                        sp.dma_start(ks[row:row + parts * HD, sl],
                                     k_scr[0:parts, :, bass.ds(at, KWIN)].rearrange("a d w -> (a d) w")
                                     ).then_inc(s_k[sl], 16)
                        row += parts * HD
                    sp.dma_start(ks[KROWS:KALL, sl], edge_rows[:, bass.ds(at, KWIN)]).then_inc(s_k[sl], 16)
                if there(vb, BLOCKS):
                    sl = (u - 1) % 4
                    wait(sp, s_pv, vb - 3)
                    at = vb * P + (vb // BPS) * (LP - SEQ)
                    for g in range(GROUPS):
                        sp.dma_start(vm[:, sl, g], v_scr[bass.ds(at + g * GQ, P), :]).then_inc(s_v[sl], 16)
                    sp.dma_start(vx[:, sl], v_scr[bass.ds(at + P, P), :]).then_inc(s_v[sl], 16)
                if there(xb_, BLOCKS):
                    sl = (u - 2) % 4
                    wait(sp, s_x2, xb_ - 3)
                    sp.dma_start(xr[:, sl], x[bass.ds(xb_ * P, P), :]).then_inc(s_xin[sl], 16)
                if there(m, BLOCKS):
                    sl = (u - 2) % 4
                    wait(sp, s_mt, m + 1)
                    for k in range(PARTS):
                        sp.dma_start(qs[KEDGE + k:KEDGE + k + 1, sl].rearrange("o g h q -> o (g h q)"),
                                     mt[k * 16:(k + 1) * 16, u % 2]).then_inc(s_m[sl], 16)
                if there(e, BLOCKS):
                    par = (u - 5) % 2
                    wait(sp, s_ob, e + 1)
                    sp.dma_start(out[bass.ds(e * P, P), :], ob[:, par]).then_inc(s_out[par], 16)

            for n in range(8):
                p2(n, n % 4)
            with sp.Fori(2, BLOCKS // 4) as t:
                for u in range(4):
                    p2(4 * t + u, u)
            for n in range(BLOCKS, BLOCKS + 5):
                p2(n, n % 4)
            for par in range(2):
                sp.wait_ge(s_out[par], 16 * BLOCKS // 2)

        @block.tensor
        def _(pe):
            pe.wait_ge(s_const, CONST)
            pe.matmul(bank[4][0:RANK, 0:WIDTH], downT[:], daux[:], start=True, stop=True).then_inc(s_low, 1)
            pe.wait_ge(s_lowc, 1)
            pe.matmul(bank[4][0:UDIM, 0:WIDTH], upT[:], low1[:], start=True, stop=True).then_inc(s_low, 1)
            pe.wait_ge(s_lowc, 2)
            for c in range(FC):
                mm = pe.matmul(bank[4][:, c * WIDTH:(c + 1) * WIDTH], low2[:, c * P:(c + 1) * P], uauxT[:],
                               start=True, stop=True)
            mm.then_inc(s_low, 1)

            def p1(s, par):
                tr, pj, vt = s + 1, s, s - 1
                if there(tr, TILES):
                    wait(pe, s_xn, tr + 1)
                    wait(pe, s_xnT, tr * FC)
                    for c in range(FC):
                        for j in range(TJ):
                            mm = pe.transpose(bank[c][:, j * P:(j + 1) * P],
                                              xn[:, 1 - par, j, c * P:(c + 1) * P], idf[:])
                        mm.then_inc(s_tr1, 1)
                if there(vt, TILES):
                    wait(pe, s_kvs, vt + 1)
                    wait(pe, s_vn, vt)
                    for j in range(TJ):
                        mm = pe.transpose(bank[3][:, j * P:(j + 1) * P], kvS[:, j * P:(j + 1) * P], idf[:])
                    mm.then_inc(s_vt, 1)
                if there(pj, TILES):
                    wait(pe, s_xnT, (pj + 1) * FC)
                    wait(pe, s_qr, pj)
                    for h in range(FC):
                        for c in range(FC):
                            mm = pe.matmul(qbank[:, h], wq[:, c, h * P:(h + 1) * P], xnT[:, par, c],
                                           start=(c == 0), stop=(c == FC - 1))
                    mm.then_inc(s_q, 1)
                    wait(pe, s_kvs, pj)
                    for c in range(FC):
                        mm = pe.matmul(bank[2][:, :], wkv[:, c], xnT[:, par, c],
                                       start=(c == 0), stop=(c == FC - 1))
                    mm.then_inc(s_kv, 1)

            p1_loop(pe, p1)

            pe.wait_ge(s_xnT, FC * TILES)
            pe.wait_ge(s_qr, TILES)
            pe.wait_ge(s_vn, TILES)
            pe.wait_ge(s_weff, 1)

            def scores(n, u, j):
                g, hp = j // 2, j % 2
                tile = sbank[j % 2]
                wait(pe, s_mx, UNITS * n + j - 1)
                for k in range(2):
                    h = 8 * hp + 4 * k
                    pe.matmul(tile[:, k * GWIN:(k + 1) * GWIN], qs[0:KEDGE, u, g, h:h + 4],
                              ks[0:KEDGE, u, g * GQ:g * GQ + GWIN], start=(k == 0), stop=False,
                              skip_group_check=True)
                dst = tile[:, 0:2 * GWIN].rearrange("p (k s c) -> p k s c", k=2, c=GQ)[:, :, 0:5:4, :]
                pe.matmul(dst, hot[:], corner[:], start=False, stop=True, skip_group_check=True).then_inc(s_sc, 1)

            def scores_t(n, u, j):
                tile = tbank[(STU * u + j) % 2]
                if j == 0:
                    wait(pe, s_m[u], 16 * M_DMAS * (n // 4 + 1))
                wait(pe, s_ex, STU * n + j - 1)
                if j < GROUPS:
                    pe.matmul(tile[:, :], ks[0:KALL, u, j * GQ:j * GQ + P], qs[0:KALL, u, j],
                              start=True, stop=True).then_inc(s_stp, 1)
                else:
                    for g in range(GROUPS):
                        at = P + g * GQ
                        pe.matmul(tile[g * GQ:(g + 1) * GQ, :], ks[0:KALL, u, at:at + GQ],
                                  qs[0:KALL, u, g], start=True, stop=False,
                                  skip_group_check=True)
                    pe.matmul(tile[:, :], remm[:], hotc[:], start=False, stop=True,
                              skip_group_check=True).then_inc(s_stp, 1)

            def times_v(n, u, last):
                par = u % 2
                if last:
                    wait(pe, s_ex, STU * (n + 1))
                    wait(pe, s_vbd, n + 1)
                else:
                    wait(pe, s_ot, n)
                    wait(pe, s_v[u], 16 * 5 * (n // 4 + 1))
                    wait(pe, s_sel, 2 * (n + 1))
                for g in range(GROUPS):
                    for j in range(4):
                        src = pr[:, par] if last else pm[:, par, g]
                        w = vbd[:, par, g] if last else vm[:, u, g]
                        dst = pvbank[j * 32:(j + 1) * 32, :].rearrange("p (h t) -> p h t", h=4)
                        mm = pe.matmul(dst[:, :, g * GQ:(g + 1) * GQ], w, src[:, j * P:(j + 1) * P],
                                       start=(not last and g == 0), stop=(last == 1 and g == GROUPS - 1),
                                       skip_group_check=True)
                if last:
                    mm.then_inc(s_pv, 1)

            def p2(n, u):
                m, c, b, e = n - 1, n - 2, n - 3, n - 4
                um, uc, ub, ue = ((u - k) % 4 for k in (1, 2, 3, 4))

                def s(*units):
                    if there(n, BLOCKS):
                        for j in units:
                            scores(n, u, j)

                def st(j):
                    if there(c, BLOCKS):
                        scores_t(c, uc, j)

                if there(n, BLOCKS):
                    wait(pe, s_qs, n + 1)
                    wait(pe, s_k[u], 16 * K_DMAS * (n // 4 + 1))
                s(0)
                if there(b, BLOCKS):
                    times_v(b, ub, 0)
                s(1)
                if there(b, BLOCKS):
                    times_v(b, ub, 1)
                if there(m, BLOCKS):
                    wait(pe, s_mp, m + 1)
                    wait(pe, s_onT, m - 2)
                    wait(pe, s_mt, m)
                    pe.transpose(trbank[:, 0:P // 2].bitcast(BF16), mp[:].rearrange("p a c -> p (a c)"),
                                 idb[:]).then_inc(s_mtp, 1)
                st(0)
                s(2)
                if there(e, BLOCKS):
                    wait(pe, s_x2n, e + 1)
                    wait(pe, s_mt, seen(e + 4))
                    for k in range(FC):
                        mm = pe.transpose(trbank[:, k * P:(k + 1) * P], x2n[:, k * P:(k + 1) * P], idf[:])
                    mm.then_inc(s_xtp, 1)
                st(1)
                s(3)
                if there(b, BLOCKS):
                    wait(pe, s_ot, b + 1)
                    wait(pe, s_on, b)
                    for k in range(4):
                        mm = pe.transpose(otbank[:, k * P:(k + 1) * P], ot[:, k * P:(k + 1) * P], idf[:])
                    mm.then_inc(s_otp, 1)
                st(2)
                s(4)
                if there(e, BLOCKS):
                    wait(pe, s_x2nT, e + 1)
                    wait(pe, s_x2, e + 1)
                    for k in range(FC):
                        mm = pe.matmul(dbank[:, 0:WIDTH], x2nT[:, k], weff[:, k], start=(k == 0),
                                       stop=(k == FC - 1))
                    mm.then_inc(s_ffn, 1)
                if there(b, BLOCKS):
                    wait(pe, s_on, b + 1)
                    wait(pe, s_x2nT, b)
                    wait(pe, s_mt, seen(b + 3))
                    for k in range(FC):
                        mm = pe.transpose(trbank[:, k * P:(k + 1) * P], on[:, k * P:(k + 1) * P], idf[:])
                    mm.then_inc(s_ntp, 1)
                st(3)
                s(5, 6)
                if there(b, BLOCKS):
                    wait(pe, s_onT, b + 1)
                    wait(pe, s_ob, b)
                    for k in range(FC):
                        mm = pe.matmul(dbank[:, 0:WIDTH], onT[:, k], wf[:, k], start=(k == 0),
                                       stop=(k == FC - 1))
                    mm.then_inc(s_wf, 1)
                st(4)
                s(7)

            p2_loop(pe, p2)

        @block.scalar
        def _(act):
            act.wait_ge(s_low, 1)
            act.copy(low1[:], bank[4][0:RANK, 0:WIDTH]).then_inc(s_lowc, 1)
            act.wait_ge(s_low, 2)
            act.copy(low2[:], bank[4][0:UDIM, 0:WIDTH]).then_inc(s_lowc, 1)

            def p1(s, par):
                tr, pj = s + 1, s
                if there(tr, TILES):
                    wait(act, s_kv, tr - 1)
                    for c in range(FC):
                        wait(act, s_tr1, tr * FC + c + 1)
                        act.copy(xnT[:, 1 - par, c], bank[c][:, :]).then_inc(s_xnT, 1)
                if there(pj, TILES):
                    wait(act, s_stq[par], 5 * 16 * (pj // 2))
                    wait(act, s_q, pj + 1)
                    act.copy(qp[:, par, 0], qbank[:, :, :]).then_inc(s_q1, 1)
                    wait(act, s_kv, pj + 1)
                    wait(act, s_vt, pj)
                    wait(act, s_kr, pj)
                    act.copy(kvS[:], bank[2][:, :]).then_inc(s_kvs, 1)
                    wait(act, s_qr, pj + 1)
                    act.copy(qp[:, par, 1], qr[:]).then_inc(s_q2, 1)
                    wait(act, s_kvs, pj + 1)
                    act.copy(kp[:, par, 0], kvS[0:HD, :]).then_inc(s_k1, 1)
                    wait(act, s_kr, pj + 1)
                    act.copy(kp[:, par, 1], kr[:]).then_inc(s_k2, 1)

            p1_loop(act, p1)

            def exps(n, u, j):
                par = u % 2
                wait(act, s_stp, STU * n + j + 1)
                if j == 0:
                    wait(act, s_pv, n - 1)
                dst = pm[:, par, j] if j < GROUPS else pr[:, par]
                act.activation(dst, tbank[(STU * u + j) % 2][:, :], ACT.Exp, scale=SCALE).then_inc(s_ex, 1)

            def p2(n, u):
                m, c, b, e = n - 1, n - 2, n - 3, n - 4
                uc = (u - 2) % 4

                def ex(*units):
                    if there(c, BLOCKS):
                        for j in units:
                            exps(c, uc, j)

                if there(b, BLOCKS):
                    wait(act, s_pv, b + 1)
                    wait(act, s_otp, b)
                    act.copy(ot[:], pvbank[:, :]).then_inc(s_ot, 1)
                if there(m, BLOCKS):
                    wait(act, s_mtp, m + 1)
                    wait(act, s_m[(u - 3) % 4], 16 * M_DMAS * ((m - 2) // 4 + 1))
                    act.copy(mt[:, (u - 1) % 2], trbank[0:PARTS * 16, 0:P // 2].bitcast(BF16)).then_inc(s_mt, 1)
                ex(0)
                if there(e, BLOCKS):
                    wait(act, s_xtp, e + 1)
                    wait(act, s_ffn, e)
                    act.copy(x2nT[:].rearrange("p c t -> p (c t)"), trbank[:, 0:WIDTH]).then_inc(s_x2nT, 1)
                ex(1, 2)
                if there(b, BLOCKS):
                    wait(act, s_ntp, b + 1)
                    wait(act, s_wf, b)
                    act.copy(onT[:].rearrange("p c t -> p (c t)"), trbank[:, 0:WIDTH]).then_inc(s_onT, 1)
                ex(3, 4)

            p2_loop(act, p2)

        @block.vector
        def _(dve):
            dve.memset(zero[:], 0.0).then_inc(s_zero, 1)
            dve.memset(neghalf[:], -0.5)
            dve.memset(bdmask[:], 0.0)
            dve.memset(vn[:], 0.0)
            dve.memset(mp[:], 0.0)
            dve.memset(qs[KROWS:KALL], 1.0).then_inc(s_set, 1)
            dve.wait_ge(s_set, 1)
            dve.memset(vn[:, :, :, HD:HD + 1], 1.0)
            for g in range(GROUPS):
                last = dve.memset(bdmask[g * GQ:(g + 1) * GQ, g], 1.0)
            last.then_inc(s_set, 1)
            dve.wait_ge(s_const, CONST)
            dve.wait_ge(s_low, 3)
            dve.tensor_tensor(weff[:].rearrange("p c n -> p (c n)"), bank[4][:, :],
                              wffn[:].rearrange("p c n -> p (c n)"), ALU.add).then_inc(s_weff, 1)

            def p1(s, par):
                ln, pj, vt = s + 2, s, s - 1
                if there(ln, TILES):
                    wait(dve, s_x1[par], 16 * (ln // 2 + 1))
                    wait(dve, s_mv1, TJ * ln)
                    for j in range(TJ):
                        dve.bn_stats(st1[:, j], xt[:, par, j]).then_inc(s_st1, 1)
                    wait(dve, s_st1, TJ * (ln + 1))
                    wait(dve, s_xn, ln)
                    dve.memset(tick[:], 0.0)
                    for j in range(TJ):
                        dve.bn_aggr(mv1[:, j], st1[:, j]).then_inc(s_mv1, 1)
                    wait(dve, s_mv1, TJ * (ln + 1))
                    wait(dve, s_rs1, ln)
                    dve.tensor_scalar(ve1[:], mv1[:, :, 1], EPS, None, ALU.add).then_inc(s_ve1, 1)
                if there(pj, TILES):
                    wait(dve, s_q1, pj + 1)
                    wait(dve, s_q3, pj)
                    dve.tensor_tensor(qr[:], qbank[:, :, :], qp[:, par, 0], ALU.subtract).then_inc(s_qr, 1)
                if there(ln, TILES):
                    wait(dve, s_rs1, ln + 1)
                    wait(dve, s_tr1, FC * (ln - 1))
                    for j in range(TJ):
                        last = dve.tensor_scalar(xn[:, par, j], xt[:, par, j], mv1[:, j, 0:1], rs1[:, j:j + 1],
                                                 ALU.subtract, ALU.mult)
                    last.then_inc(s_xn, 1)
                if there(pj, TILES):
                    wait(dve, s_q2, pj + 1)
                    dve.tensor_tensor(qp[:, par, 2], qr[:], qp[:, par, 1], ALU.subtract).then_inc(s_q3, 1)
                if there(vt, TILES):
                    wait(dve, s_vt, vt + 1)
                    wait(dve, s_stq[1 - par], 5 * 16 * (vt // 2))
                    dve.tensor_copy(vn[:, 1 - par, :, 0:HD],
                                    bank[3].rearrange("p (j c) -> p j c", c=P)[:, :, 32:32 + HD]
                                    ).then_inc(s_vn, 1)

            p1_loop(dve, p1)

            def p2(n, u):
                b, e = n - 3, n - 4
                par = u % 2

                def mx_(*units):
                    if there(n, BLOCKS):
                        for j in units:
                            wait(dve, s_sc, UNITS * n + j + 1)
                            dve.tensor_reduce(mx[:, par, 2 * j:2 * j + 2],
                                              sbank[j % 2][:, 0:2 * GWIN].rearrange("p (k c) -> p k c", k=2),
                                              AX.X, ALU.max).then_inc(s_mx, 1)

                mx_(0, 1, 2, 3)
                if there(b, BLOCKS):
                    wait(dve, s_otp, b + 1)
                    o4 = otbank.rearrange("p (hh j d) -> p hh j d", hh=4, j=4)
                    dve.reciprocal(rden[:], o4[:, :, :, HD]).then_inc(s_rd, 1)
                    wait(dve, s_rd, b + 1)
                    wait(dve, s_ntp, b)
                    dve.tensor_tensor(on[:].rearrange("p (j hh d) -> p hh j d", j=4, hh=4), o4[:, :, :, 0:HD],
                                      rden[:].unsqueeze(3).to_broadcast([P, 4, 4, HD]), ALU.mult
                                      ).then_inc(s_on, 1)
                mx_(4)
                if there(e, BLOCKS):
                    wait(dve, s_ffn, e + 1)
                    wait(dve, s_x2b, e + 1)
                    wait(dve, s_out[u % 2], 16 * (e // 2))
                    dve.tensor_tensor(ob[:, u % 2], dbank[:, 0:WIDTH], x2b[:], ALU.add).then_inc(s_ob, 1)
                a = n + 1
                if there(a, BLOCKS):
                    v = (u + 1) % 4
                    wait(dve, s_qin[v // 2], 16 * Q_DMAS * (a // 4 + 1))
                    wait(dve, s_stp, STU * (a - 3))
                    at = (v % 2) * P
                    dve.tensor_copy(qs[0:KROWS, v], qin[:, v // 2, :, at:at + P].rearrange(
                        "p h (g q) -> p g h q", q=GQ)).then_inc(s_qs, 1)
                mx_(5)
                if there(b, BLOCKS):
                    wait(dve, s_wf, b + 1)
                    wait(dve, s_xb, b + 1)
                    wait(dve, s_x2b, b)
                    dve.tensor_tensor(x2[:], dbank[:, 0:WIDTH], xr[:, (u - 3) % 4], ALU.add).then_inc(s_x2, 1)
                mx_(6)
                if there(b, BLOCKS):
                    wait(dve, s_x2, b + 1)
                    dve.bn_stats(st2[:], x2[:]).then_inc(s_st2, 1)
                mx_(7)
                if there(b, BLOCKS):
                    wait(dve, s_st2, b + 1)
                    dve.memset(tick[:], 0.0)
                    dve.bn_aggr(mv2[:], st2[:]).then_inc(s_mv2, 1)
                if there(n, BLOCKS):
                    wait(dve, s_mx, UNITS * (n + 1))
                    wait(dve, s_mtp, n)
                    m_ = mx[:, par]
                    dve.tensor_copy(mp[:, 0], m_).then_inc(s_mp1, 1)
                if there(b, BLOCKS):
                    wait(dve, s_mv2, b + 1)
                    dve.tensor_scalar(ve2[:], mv2[:, 1:2], EPS, None, ALU.add).then_inc(s_ve2, 1)
                if there(n, BLOCKS):
                    wait(dve, s_mp1, n + 1)
                    dve.tensor_tensor(mr[:, 0], m_, mp[:, 0], ALU.subtract).then_inc(s_mr1, 1)
                    wait(dve, s_mr1, n + 1)
                    dve.tensor_copy(mp[:, 1], mr[:, 0]).then_inc(s_mp2, 1)
                    wait(dve, s_mp2, n + 1)
                    dve.tensor_tensor(mp[:, 2], mr[:, 0], mp[:, 1], ALU.subtract).then_inc(s_mp, 1)
                if there(b, BLOCKS):
                    wait(dve, s_rs2, b + 1)
                    wait(dve, s_xtp, b)
                    dve.tensor_scalar(x2n[:], x2[:], mv2[:, 0:1], rs2[:], ALU.subtract, ALU.mult
                                      ).then_inc(s_x2n, 1)

            p2_loop(dve, p2)

        @block.gpsimd
        def _(pool):
            pool.wait_ge(s_const, CONST)
            pool.wait_ge(s_set, 2)

            def p1(s, par):
                ln, pj = s + 2, s
                if there(ln, TILES):
                    wait(pool, s_ve1, ln + 1)
                    wait(pool, s_xn, ln)
                    pool.tensor_tensor(rs1[:], ve1[:], neghalf[:], ALU.pow).then_inc(s_rs1, 1)
                if there(pj, TILES):
                    wait(pool, s_k1, pj + 1)
                    wait(pool, s_k3, pj)
                    pool.tensor_tensor(kr[:], kvS[0:HD, :], kp[:, par, 0], ALU.subtract).then_inc(s_kr, 1)
                    wait(pool, s_k2, pj + 1)
                    pool.tensor_tensor(kp[:, par, 2], kr[:], kp[:, par, 1], ALU.subtract).then_inc(s_k3, 1)

            p1_loop(pool, p1)

            def p2(n, u):
                c, b = n - 2, n - 3
                uc = (u - 2) % 4

                def select(g):
                    v = pm[0:GQ, uc % 2, g:g + 2].rearrange("p g (h q) -> p (g h) q", h=HEADS)
                    pool.affine_select(out=v, in_=v, compare_op=ALU.is_ge, fill=0.0, base=0,
                                       pattern=[[0, 2 * HEADS], [-1, GQ]], channel_multiplier=1
                                       ).then_inc(s_sel, 1)

                if there(c, BLOCKS):
                    wait(pool, s_v[uc], 16 * 5 * (c // 4 + 1))
                    wait(pool, s_pv, c - 1)
                    wait(pool, s_ex, STU * c + 2)
                    pool.tensor_tensor(vbd[:, uc % 2], vx[:, uc].unsqueeze(1).to_broadcast([P, GROUPS, VW]),
                                       bdmask[:], ALU.mult).then_inc(s_vbd, 1)
                    select(0)
                    wait(pool, s_xin[uc], 16 * (c // 4 + 1))
                    wait(pool, s_ex, STU * c + 4)
                    pool.tensor_tensor(xr[:, uc], xr[:, uc], bf_bc[:], ALU.add).then_inc(s_xb, 1)
                    select(2)
                if there(b, BLOCKS):
                    wait(pool, s_ve2, b + 1)
                    wait(pool, s_x2n, b)
                    pool.tensor_tensor(rs2[:], ve2[:], neghalf[:, 0:1], ALU.pow).then_inc(s_rs2, 1)
                    wait(pool, s_x2, b + 1)
                    wait(pool, s_ob, b)
                    pool.tensor_tensor(x2b[:], x2[:], b_bc[:], ALU.add).then_inc(s_x2b, 1)

            p2_loop(pool, p2)


def kernel(L0_attn_x, L0_attn_Wq, L0_attn_Wk, L0_attn_Wv, L0_attn_Wf, L0_attn_bf, L0_ffn_W, L0_ffn_b,
           L0_ffn_lora_down, L0_ffn_lora_up, L0_ffn_down_aux, L0_ffn_up_aux):
    import ml_dtypes
    import numpy as np
    import concourse.bacc as bacc
    from concourse.bass_utils import run_bass_kernel_spmd

    bf = ml_dtypes.bfloat16
    f = np.float32
    wkv = np.zeros((WIDTH, P), f)
    wkv[:, 0:HD] = np.asarray(L0_attn_Wk).T
    wkv[:, 32:32 + HD] = np.asarray(L0_attn_Wv).T
    edge = np.zeros((1 + PARTS, BATCH, LP), f)
    edge[0, :, 0:WINDOW] = NEG
    edge[0, :, WINDOW + SEQ:] = NEG
    edge[1:] = -1.0
    i = np.arange(GQ)
    onehot = np.tile(np.eye(GQ, dtype=f), (1, P // GQ))
    corner = np.zeros((GQ, 2, 2, GQ), f)
    corner[:, :, 0] = np.where(i[None, :] < i[:, None], NEG, 0.0)[:, None, :]
    corner[:, :, 1] = np.where(i[None, :] > i[:, None], NEG, 0.0)[:, None, :]
    rem = np.tile(np.where(i[None, :] > i[:, None], NEG, 0.0), (1, GROUPS))
    data = {
        "x": np.asarray(L0_attn_x).reshape(TOKENS, WIDTH),
        "wq_t": np.asarray(L0_attn_Wq).T, "wkv_t": wkv, "wf_t": np.asarray(L0_attn_Wf).T,
        "bf_rows": np.broadcast_to(np.asarray(L0_attn_bf), (P, WIDTH)),
        "wffn_t": np.asarray(L0_ffn_W).T, "b_rows": np.broadcast_to(np.asarray(L0_ffn_b), (P, WIDTH)),
        "down_t": np.asarray(L0_ffn_lora_down).T, "up_t": np.asarray(L0_ffn_lora_up).T,
        "down_aux": np.asarray(L0_ffn_down_aux), "up_aux_t": np.asarray(L0_ffn_up_aux).T,
        "edge_rows": edge.reshape(1 + PARTS, BATCH * LP).astype(bf),
        "onehot": onehot.astype(bf), "corners": corner.astype(bf), "rem_mask": rem.astype(bf),
        "onehot_cols": np.tile(np.eye(GQ, dtype=f), (1, HEADS)).astype(bf),
        "ident": np.eye(P, dtype=f), "ident_b": np.eye(P, dtype=f).astype(bf),
    }
    nc = bacc.Bacc("TRN2", target_bir_lowering=False, num_devices=1)
    arrays, args = {}, []
    for name, a in data.items():
        arrays[f"in_{name}"] = a = np.ascontiguousarray(a)
        args.append(nc.dram_tensor(f"in_{name}", a.shape, mybir.dt.from_np(a.dtype), kind="ExternalInput").ap())
    args.append(nc.dram_tensor("out_y", (TOKENS, WIDTH), F32, kind="ExternalOutput").ap())
    build(nc, *args)
    r = run_bass_kernel_spmd(nc, [arrays], core_ids=[0])
    return r.results[0]["out_y"].reshape(BATCH, SEQ, WIDTH)
```

```python
from contextlib import ExitStack

import concourse.bass as bass
from concourse import mybir

F32 = mybir.dt.float32
BF16 = mybir.dt.bfloat16
ALU = mybir.AluOpType
ACT = mybir.ActivationFunctionType
AX = mybir.AxisListType

P = 128
BATCH, SEQ, WIDTH = 4, 2048, 256
HEADS, HD = 16, 16
WINDOW = 64
TOKENS = BATCH * SEQ
TILE = 512
TILES = TOKENS // TILE
TJ = TILE // P
BLOCKS = TOKENS // P
BPS = SEQ // P
GQ = 32
GROUPS = P // GQ
GWIN = GQ + 2 * WINDOW
KWIN = P + 2 * WINDOW
LP = SEQ + 2 * WINDOW
VW = 32
KV = 2 * HD
PARTS = 3
KROWS = 6 * HD
KEDGE = KROWS + 1
KALL = KEDGE + PARTS
KSTORE = PARTS * HD + KALL - KROWS
FC = WIDTH // P
RING = 4
UNITS = 2 * GROUPS
STU = GROUPS + 1
NEG = -1.0e30
EPS = 1e-5
SCALE = HD ** -0.5
DDIM, UDIM, RANK = 100, 50, 4

S_DMAS = PARTS + TJ
K_DMAS = 3
Q_DMAS = 6


def wait(engine, semaphore, value):
    if isinstance(value, int) and value <= 0:
        return
    engine.wait_ge(semaphore, value)


def there(i, n):
    return not isinstance(i, int) or 0 <= i < n


def seen(count):
    return min(count, BLOCKS) if isinstance(count, int) else count


def build(nc, x, wq_t, wkv_t, wf_t, bf_rows, wffn_t, b_rows, down_t, up_t, down_aux, up_aux_t,
          edge_rows, onehot, corners, rem_mask, onehot_cols, ident, ident_b, out):
    q_scr = nc.dram_tensor("q_scratch", (PARTS, WIDTH, TOKENS), BF16, kind="Internal").ap()
    k_scr = nc.dram_tensor("k_scratch", (KSTORE, BATCH * LP), BF16, kind="Internal").ap()
    v_scr = nc.dram_tensor("v_scratch", (BATCH * LP, VW), F32, kind="Internal").ap()

    ctx = ExitStack()
    with ctx:
        def sb(name, shape, dt=F32):
            return ctx.enter_context(nc.sbuf_tensor(name, shape, dt))

        def sem(name):
            return ctx.enter_context(nc.semaphore(name))

        wq = sb("wq", [P, FC, WIDTH])
        wkv = sb("wkv", [P, FC, KV])
        wf = sb("wf", [P, FC, WIDTH])
        bf_bc = sb("bf_bc", [P, WIDTH])
        b_bc = sb("b_bc", [P, WIDTH])
        wffn = sb("wffn", [P, FC, WIDTH])
        weff = sb("weff", [P, FC, WIDTH])
        downT = sb("downT", [DDIM, RANK])
        upT = sb("upT", [RANK, UDIM])
        daux = sb("daux", [DDIM, WIDTH])
        uauxT = sb("uauxT", [UDIM, WIDTH])
        low1 = sb("low1", [RANK, WIDTH])
        low2 = sb("low2", [UDIM, WIDTH])
        hot = sb("hot", [GQ, P], BF16)
        corner = sb("corner", [GQ, 2, 2, GQ], BF16)
        remm = sb("remm", [GQ, P], BF16)
        hotc = sb("hotc", [GQ, HEADS * GQ], BF16)
        idf = sb("idf", [P, P])
        idb = sb("idb", [P, P], BF16)
        tick = sb("tick", [1, 1])
        ptick = sb("ptick", [1, GROUPS])
        neghalf = sb("neghalf", [P, TJ])
        bdmask = sb("bdmask", [P, GROUPS, VW])
        zero = sb("zero", [P, P])

        xt = sb("xt", [P, 2, TJ, WIDTH])
        st1 = sb("st1", [P, TJ, 6])
        mv1 = sb("mv1", [P, TJ, 2])
        ve1 = sb("ve1", [P, TJ])
        rs1 = sb("rs1", [P, TJ])
        xn = sb("xn", [P, 2, TJ, WIDTH])
        xnT = sb("xnT", [P, 2, FC, TILE])
        qp = sb("qp", [P, 2, PARTS, FC, TILE], BF16)
        qr = sb("qr", [P, FC, TILE])
        kvS = sb("kvS", [P, P])
        kp = sb("kp", [P, 2, PARTS, P], BF16)
        kr = sb("kr", [P, P])
        vn = sb("vn", [P, 2, TJ, VW])

        qin = sb("qin", [KROWS, 2, HEADS, 2 * P], BF16)
        qs = sb("qs", [KALL, RING, GROUPS, HEADS, GQ], BF16)
        ks = sb("ks", [KALL, RING, KWIN], BF16)
        vm = sb("vm", [P, RING, GROUPS + 1, VW])
        vbd = sb("vbd", [P, 2, GROUPS, VW])
        xr = sb("xr", [P, RING, WIDTH])
        mx = sb("mx", [P, 2, 16])
        mp = sb("mp", [P, P // 16, 16], BF16)
        mr = sb("mr", [P, 2, 16])
        mt = sb("mt", [PARTS * 16, 2, P], BF16)
        pm = sb("pm", [P, 2, GROUPS, HEADS * GQ])
        pr = sb("pr", [P, 2, HEADS * GQ])
        ot = sb("ot", [P, HEADS, VW])
        rden = sb("rden", [P, HEADS])
        on = sb("on", [P, WIDTH])
        onT = sb("onT", [P, FC, P])
        x2 = sb("x2", [P, WIDTH])
        st2 = sb("st2", [P, 6])
        mv2 = sb("mv2", [P, 2])
        ve2 = sb("ve2", [P, 1])
        rs2 = sb("rs2", [P, 1])
        x2n = sb("x2n", [P, WIDTH])
        x2nT = sb("x2nT", [P, FC, P])
        x2b = sb("x2b", [P, WIDTH])
        ob = sb("ob", [P, 4, WIDTH])

        bank = [ctx.enter_context(nc.psum_tensor(f"bank{i}", [P, 512], F32)) for i in range(5)]
        qbank = ctx.enter_context(nc.psum_tensor("qbank", [P, FC, 512], F32))
        b7 = ctx.enter_context(nc.psum_tensor("bank7", [P, 512], F32))
        sbank, tbank, pvbank, xtbank, trbank, dbank = bank[0:2], bank[2:4], bank[4], qbank[:, 0], qbank[:, 1], b7

        s_early = sem("s_early")
        s_const = sem("s_const")
        s_set = sem("s_set")
        s_zero = sem("s_zero")
        s_halo = sem("s_halo")
        s_low = sem("s_low")
        s_lowc = sem("s_lowc")
        s_weff = sem("s_weff")

        s_x1 = [sem(f"s_x1_{i}") for i in range(2)]
        s_st1, s_mv1, s_ve1, s_rs1, s_xn = (sem(n) for n in ("s_st1", "s_mv1", "s_ve1", "s_rs1", "s_xn"))
        s_tr1, s_xnT, s_q, s_kv, s_vt = (sem(n) for n in ("s_tr1", "s_xnT", "s_q", "s_kv", "s_vt"))
        s_q1, s_qr, s_q2, s_q3 = (sem(n) for n in ("s_q1", "s_qr", "s_q2", "s_q3"))
        s_kvs, s_k1, s_kr, s_k2, s_k3, s_vn = (sem(n) for n in ("s_kvs", "s_k1", "s_kr", "s_k2", "s_k3", "s_vn"))
        s_stq = [sem(f"s_stq{i}") for i in range(2)]
        s_stv = [sem(f"s_stv{i}") for i in range(2)]

        s_qin = [sem(f"s_qin{i}") for i in range(2)]
        s_qs = sem("s_qs")
        s_k = [sem(f"s_k_{i}") for i in range(RING)]
        s_v = [sem(f"s_v{i}") for i in range(RING)]
        s_xin = [sem(f"s_xin{i}") for i in range(RING // 2)]
        s_m = [sem(f"s_m{i}") for i in range(RING)]
        s_out = [sem(f"s_out{i}") for i in range(2)]
        s_sc, s_mx, s_mp1, s_mr1, s_mp2, s_mr2, s_mp = (sem(n) for n in (
            "s_sc", "s_mx", "s_mp1", "s_mr1", "s_mp2", "s_mr2", "s_mp"))
        s_mtp, s_mt = sem("s_mtp"), sem("s_mt")
        s_stp, s_ex, s_sel, s_vbd = (sem(n) for n in ("s_stp", "s_ex", "s_sel", "s_vbd"))
        s_pv, s_ot, s_rd, s_on = (sem(n) for n in ("s_pv", "s_ot", "s_rd", "s_on"))
        s_ntp, s_onT, s_wf, s_xb, s_x2, s_st2, s_mv2, s_ve2, s_rs2 = (sem(n) for n in (
            "s_ntp", "s_onT", "s_wf", "s_xb", "s_x2", "s_st2", "s_mv2", "s_ve2", "s_rs2"))
        s_x2n, s_xtp, s_x2nT, s_ffn, s_x2b, s_ob = (sem(n) for n in (
            "s_x2n", "s_xtp", "s_x2nT", "s_ffn", "s_x2b", "s_ob"))

        consts = [
            (idf[:], ident), (wkv[:], wkv_t.rearrange("(c p) n -> p c n", p=P)),
            (wq[:], wq_t.rearrange("(c p) n -> p c n", p=P)),
            (wf[:], wf_t.rearrange("(c p) n -> p c n", p=P)), (wffn[:], wffn_t.rearrange("(c p) n -> p c n", p=P)),
            (bf_bc[:], bf_rows), (b_bc[:], b_rows), (downT[:], down_t), (upT[:], up_t), (daux[:], down_aux),
            (uauxT[:], up_aux_t), (hot[:], onehot), (corner[:], corners), (remm[:], rem_mask),
            (hotc[:], onehot_cols), (idb[:], ident_b),
        ]
        EARLY = 3

        block = ctx.enter_context(nc.Block())

        def p1_loop(engine, step, end=TILES + 1):
            for s in range(-2, 4):
                step(s, s % 2)
            with engine.Fori(2, TILES // 2 - 2) as i:
                for u in range(2):
                    step(2 * i + u, u)
            for s in range(TILES - 4, end):
                step(s, s % 2)

        def p2_loop(engine, step):
            for n in range(-1, 8):
                step(n, n % 4)
            with engine.Fori(2, BLOCKS // 4 - 1) as t:
                for u in range(4):
                    step(4 * t + u, u)
            for n in range(BLOCKS - 4, BLOCKS + 5):
                step(n, n % 4)

        @block.sync
        def _(sp):
            def load_x(ld, par):
                sp.dma_start(xt[:, par], x[bass.ds(ld * TILE, TILE), :].rearrange("(j p) f -> p j f", p=P)
                             ).then_inc(s_x1[par], 16)

            load_x(0, 0)
            for dst, src in consts[:EARLY]:
                sp.dma_start(dst, src).then_inc(s_early, 16)
            load_x(1, 1)
            for dst, src in consts[EARLY:]:
                sp.dma_start(dst, src).then_inc(s_const, 16)
            sp.wait_ge(s_zero, 1)
            sp.dma_start(k_scr[PARTS * HD:KSTORE, :], edge_rows).then_inc(s_halo, 16)
            n_halo = 16
            for b in range(BATCH):
                for at in (b * LP, b * LP + WINDOW + SEQ):
                    sp.dma_start(k_scr[0:PARTS * HD, at:at + WINDOW], zero[0:PARTS * HD, 0:WINDOW // 2].bitcast(BF16)
                                 ).then_inc(s_halo, 16)
                    sp.dma_start(v_scr[at:at + WINDOW, :], zero[0:WINDOW, 0:VW]).then_inc(s_halo, 16)
                    n_halo += 32

            def p1(s, par):
                ld, pj, vt = s + 4, s, s - 1
                if there(ld, TILES):
                    wait(sp, s_xn, ld - 1)
                    load_x(ld, par)
                if there(pj, TILES):
                    wait(sp, s_q3, FC * (pj + 1))
                    for a in range(PARTS):
                        sp.dma_start(q_scr[a, :, bass.ds(pj * TILE, TILE)].rearrange("(c p) t -> p c t", p=P),
                                     qp[:, par, a]).then_inc(s_stq[par], 16)
                    wait(sp, s_k3, pj + 1)
                    at = pj * TILE + (pj // 4) * (LP - SEQ) + WINDOW
                    for j in range(TJ):
                        sp.dma_start(k_scr[0:PARTS * HD, bass.ds(at + j * P, P)].rearrange("(a d) t -> d a t", d=HD),
                                     kp[j * KV:j * KV + HD, par]).then_inc(s_stq[par], 16)
                if there(vt, TILES):
                    wait(sp, s_vn, vt + 1)
                    at = vt * TILE + (vt // 4) * (LP - SEQ) + WINDOW
                    sp.dma_start(v_scr[bass.ds(at, TILE), :].rearrange("(j p) c -> p j c", p=P),
                                 vn[:, 1 - par]).then_inc(s_stv[1 - par], 16)

            def p2(n, u):
                a, vb, xb_, m, e = n, n - 1, n - 2, n - 2, n - 5
                if u % 2 == 0 and there(a, BLOCKS):
                    wait(sp, s_qs, GROUPS * (a - 2))
                    row = 0
                    for part, copies in ((0, 3), (1, 2), (2, 1)):
                        for _ in range(copies):
                            sp.dma_start(qin[row:row + HD, u // 2],
                                         q_scr[part, :, bass.ds(a * P, 2 * P)].rearrange("(h d) t -> d h t", d=HD)
                                         ).then_inc(s_qin[u // 2], 16)
                            row += HD
                if there(a, BLOCKS):
                    wait(sp, s_stp, STU * (a - 3))
                    sl = u
                    at = a * P + (a // BPS) * (LP - SEQ)
                    for row, k_row, rows in ((0, 0, 3 * HD), (3 * HD, HD, 2 * HD), (5 * HD, 2 * HD, KSTORE - 2 * HD)):
                        sp.dma_start(ks[row:row + rows, sl], k_scr[k_row:k_row + rows, bass.ds(at, KWIN)]
                                     ).then_inc(s_k[sl], 16)
                if there(vb, BLOCKS):
                    sl = (u - 1) % 4
                    wait(sp, s_pv, vb - 3)
                    at = vb * P + (vb // BPS) * (LP - SEQ)
                    row = v_scr[bass.ds(at, P), :]
                    sp.dma_start(vm[:, sl], bass.AP(row.tensor, row.offset, [[VW, P], [GQ * VW, GROUPS + 1], [1, VW]])
                                 ).then_inc(s_v[sl], 16)
                if u % 2 == 0 and there(xb_, BLOCKS):
                    sl = (u - 2) % 4
                    wait(sp, s_x2, xb_ - 2)
                    sp.dma_start(xr[:, sl:sl + 2], x[bass.ds(xb_ * P, 2 * P), :].rearrange(
                        "(i p) f -> p i f", p=P)).then_inc(s_xin[sl // 2], 16)
                if there(m, BLOCKS):
                    sl = (u - 2) % 4
                    wait(sp, s_mt, m + 1)
                    sp.dma_start(qs[KEDGE:KALL, sl].rearrange("o g h q -> o (g h q)"), mt[:, u % 2]
                                 ).then_inc(s_m[sl], 16)
                if u % 2 == 0 and there(e, BLOCKS):
                    sl = (u - 6) % 4
                    wait(sp, s_ob, e + 1)
                    sp.dma_start(out[bass.ds((e - 1) * P, 2 * P), :].rearrange("(i p) f -> p i f", p=P),
                                 ob[:, sl:sl + 2]).then_inc(s_out[sl // 2], 16)

            p1_loop(sp, p1, TILES - 1)
            sp.wait_ge(s_halo, n_halo)
            sp.wait_ge(s_set, 2)
            sp.wait_ge(s_stq[0], S_DMAS * 16)
            sp.wait_ge(s_stv[0], 16)
            for n in range(2):
                p2(n, n % 4)
            for s in range(TILES - 1, TILES + 1):
                p1(s, s % 2)
            for par in range(2):
                sp.wait_ge(s_stq[par], S_DMAS * 16 * TILES // 2)
                sp.wait_ge(s_stv[par], 16 * TILES // 2)
            for n in range(2, 8):
                p2(n, n % 4)
            with sp.Fori(2, BLOCKS // 4) as t:
                for u in range(4):
                    p2(4 * t + u, u)
            for n in range(BLOCKS, BLOCKS + 5):
                p2(n, n % 4)
            for par in range(2):
                sp.wait_ge(s_out[par], 16 * BLOCKS // 4)

        @block.tensor
        def _(pe):
            pe.wait_ge(s_early, 16 * EARLY)

            def p1(s, par):
                tr, pj, vt = s + 1, s, s - 1
                def q(h):
                    if there(pj, TILES):
                        wait(pe, s_qr, FC * (pj - 1) + h + 1)
                        for c in range(FC):
                            mm = pe.matmul(qbank[:, h], wq[:, c, h * P:(h + 1) * P], xnT[:, par, c],
                                           start=(c == 0), stop=(c == FC - 1))
                        mm.then_inc(s_q, 1)

                if there(vt, TILES):
                    wait(pe, s_kvs, vt + 1)
                    wait(pe, s_vn, vt)
                    pe.transpose(bank[3][:, 0:P], kvS[:], idf[:]).then_inc(s_vt, 1)
                if there(pj, TILES):
                    wait(pe, s_xnT, (pj + 1) * FC)
                    wait(pe, s_kvs, pj)
                    for c in range(FC):
                        for j in range(TJ):
                            mm = pe.matmul(bank[2][j * KV:(j + 1) * KV, 0:P], wkv[:, c],
                                           xnT[:, par, c, j * P:(j + 1) * P], start=(c == 0), stop=(c == FC - 1),
                                           skip_group_check=True)
                    mm.then_inc(s_kv, 1)
                q(0)
                if there(tr, TILES):
                    wait(pe, s_xn, tr + 1)
                    wait(pe, s_xnT, tr * FC)
                    for c in range(FC):
                        for j in range(TJ):
                            mm = pe.transpose(bank[c][:, j * P:(j + 1) * P],
                                              xn[:, 1 - par, j, c * P:(c + 1) * P], idf[:])
                        mm.then_inc(s_tr1, 1)
                q(1)

            p1_loop(pe, p1)

            pe.wait_ge(s_const, 16 * (len(consts) - EARLY))
            pe.matmul(bank[4][0:RANK, 0:WIDTH], downT[:], daux[:], start=True, stop=True).then_inc(s_low, 1)
            pe.wait_ge(s_lowc, 1)
            pe.matmul(bank[4][0:UDIM, 0:WIDTH], upT[:], low1[:], start=True, stop=True).then_inc(s_low, 1)
            pe.wait_ge(s_lowc, 2)
            for c in range(FC):
                mm = pe.matmul(bank[4][:, c * WIDTH:(c + 1) * WIDTH], low2[:, c * P:(c + 1) * P], uauxT[:],
                               start=True, stop=True)
            mm.then_inc(s_low, 1)

            pe.wait_ge(s_xnT, FC * TILES)
            pe.wait_ge(s_qr, FC * TILES)
            pe.wait_ge(s_vn, TILES)
            pe.wait_ge(s_weff, 1)

            def scores(n, u, j):
                g, hp = j // 2, j % 2
                tile = sbank[j % 2]
                wait(pe, s_mx, UNITS * n + j - 1)
                for k in range(2):
                    h = 8 * hp + 4 * k
                    pe.matmul(tile[:, k * GWIN:(k + 1) * GWIN], qs[0:KEDGE, u, g, h:h + 4],
                              ks[0:KEDGE, u, g * GQ:g * GQ + GWIN], start=(k == 0), stop=False,
                              skip_group_check=True)
                dst = tile[:, 0:2 * GWIN].rearrange("p (k s c) -> p k s c", k=2, c=GQ)[:, :, 0:5:4, :]
                pe.matmul(dst, hot[:], corner[:], start=False, stop=True, skip_group_check=True).then_inc(s_sc, 1)

            def scores_t(n, u, j):
                tile = tbank[(STU * u + j) % 2]
                if j == 0:
                    wait(pe, s_m[u], 16 * (n // 4 + 1))
                wait(pe, s_ex, STU * n + j - 1)
                if j < GROUPS:
                    pe.matmul(tile[:, :], ks[0:KALL, u, j * GQ:j * GQ + P], qs[0:KALL, u, j],
                              start=True, stop=True).then_inc(s_stp, 1)
                else:
                    for g in range(GROUPS):
                        at = P + g * GQ
                        pe.matmul(tile[g * GQ:(g + 1) * GQ, :], ks[0:KALL, u, at:at + GQ],
                                  qs[0:KALL, u, g], start=True, stop=False,
                                  skip_group_check=True)
                    pe.matmul(tile[:, :], remm[:], hotc[:], start=False, stop=True,
                              skip_group_check=True).then_inc(s_stp, 1)

            def times_v(n, u, last):
                par = u % 2
                if last:
                    wait(pe, s_ex, STU * (n + 1))
                    wait(pe, s_vbd, n + 1)
                    pe.matmul(pvbank[:, :], vbd[:, par].rearrange("p g c -> p (g c)"), pr[:, par],
                              start=False, stop=True, skip_group_check=True).then_inc(s_pv, 1)
                else:
                    wait(pe, s_ot, n)
                    wait(pe, s_v[u], 16 * (n // 4 + 1))
                    wait(pe, s_sel, GROUPS * (n + 1))
                    for g in range(GROUPS):
                        pe.matmul(pvbank[g * VW:(g + 1) * VW, :], vm[:, u, g], pm[:, par, g],
                                  start=True, stop=False, skip_group_check=True)

            def p2(n, u):
                m, c, b, e = n - 1, n - 2, n - 3, n - 4
                um, uc, ub, ue = ((u - k) % 4 for k in (1, 2, 3, 4))

                def s(*units):
                    if there(n, BLOCKS):
                        for j in units:
                            scores(n, u, j)

                def st(j):
                    if there(c, BLOCKS):
                        scores_t(c, uc, j)

                if there(n, BLOCKS):
                    wait(pe, s_qs, GROUPS * (n + 1))
                    wait(pe, s_k[u], 16 * K_DMAS * (n // 4 + 1))
                s(0)
                if there(b, BLOCKS):
                    times_v(b, ub, 0)
                    times_v(b, ub, 1)
                s(1)
                if there(m, BLOCKS):
                    wait(pe, s_mp, m + 1)
                    wait(pe, s_onT, m - 2)
                    pe.transpose(trbank[:, 0:P // 2].bitcast(BF16), mp[:].rearrange("p a c -> p (a c)"),
                                 idb[:]).then_inc(s_mtp, 1)
                if there(e, BLOCKS):
                    wait(pe, s_x2n, e + 1)
                    wait(pe, s_x2nT, e)
                    for k in range(FC):
                        mm = pe.transpose(xtbank[:, k * P:(k + 1) * P], x2n[:, k * P:(k + 1) * P], idf[:])
                    mm.then_inc(s_xtp, 1)
                st(0)
                s(2)
                st(1)
                s(3)
                if there(e, BLOCKS):
                    wait(pe, s_x2nT, e + 1)
                    wait(pe, s_x2, e + 1)
                    for k in range(FC):
                        mm = pe.matmul(dbank[:, 0:WIDTH], x2nT[:, k], weff[:, k], start=(k == 0),
                                       stop=(k == FC - 1))
                    mm.then_inc(s_ffn, 1)
                st(2)
                if there(b, BLOCKS):
                    wait(pe, s_on, b + 1)
                    wait(pe, s_mt, seen(b + 3))
                    for k in range(FC):
                        mm = pe.transpose(trbank[:, k * P:(k + 1) * P], on[:, k * P:(k + 1) * P], idf[:])
                    mm.then_inc(s_ntp, 1)
                s(4)
                st(3)
                s(5, 6)
                if there(b, BLOCKS):
                    wait(pe, s_onT, b + 1)
                    wait(pe, s_ob, b)
                    for k in range(FC):
                        mm = pe.matmul(dbank[:, 0:WIDTH], onT[:, k], wf[:, k], start=(k == 0),
                                       stop=(k == FC - 1))
                    mm.then_inc(s_wf, 1)
                st(4)
                s(7)

            p2_loop(pe, p2)

        @block.scalar
        def _(act):
            def p1(s, par):
                tr, pj = s + 1, s
                def q1(h):
                    if there(pj, TILES):
                        wait(act, s_q, FC * pj + h + 1)
                        act.copy(qp[:, par, 0, h], qbank[:, h]).then_inc(s_q1, 1)

                if there(pj, TILES):
                    wait(act, s_kv, pj + 1)
                    wait(act, s_vt, pj)
                    wait(act, s_kr, pj)
                    act.copy(kvS[:], bank[2][:, 0:P]).then_inc(s_kvs, 1)
                    wait(act, s_stq[par], S_DMAS * 16 * (pj // 2))
                q1(0)
                if there(pj, TILES):
                    wait(act, s_kvs, pj + 1)
                    act.copy(kp[:, par, 2], kvS[:]).then_inc(s_k1, 1)
                if there(tr, TILES):
                    wait(act, s_q, FC * (tr - 1))
                    for c in range(FC):
                        wait(act, s_tr1, tr * FC + c + 1)
                        act.copy(xnT[:, 1 - par, c], bank[c][:, :]).then_inc(s_xnT, 1)
                if there(pj, TILES):
                    wait(act, s_kr, pj + 1)
                    act.copy(kp[:, par, 1], kr[:]).then_inc(s_k2, 1)
                q1(1)
                if there(pj, TILES):
                    for h in range(FC):
                        wait(act, s_qr, FC * pj + h + 1)
                        act.copy(qp[:, par, 1, h], qr[:, h]).then_inc(s_q2, 1)

            p1_loop(act, p1)

            act.wait_ge(s_low, 1)
            act.copy(low1[:], bank[4][0:RANK, 0:WIDTH]).then_inc(s_lowc, 1)
            act.wait_ge(s_low, 2)
            act.copy(low2[:], bank[4][0:UDIM, 0:WIDTH]).then_inc(s_lowc, 1)

            def exps(n, u, j):
                par = u % 2
                wait(act, s_stp, STU * n + j + 1)
                if j == 0:
                    wait(act, s_pv, n - 1)
                dst = pm[:, par, j] if j < GROUPS else pr[:, par]
                act.activation(dst, tbank[(STU * u + j) % 2][:, :], ACT.Exp, scale=SCALE).then_inc(s_ex, 1)

            def p2(n, u):
                m, c, b, e = n - 1, n - 2, n - 3, n - 4
                uc = (u - 2) % 4

                def ex(*units):
                    if there(c, BLOCKS):
                        for j in units:
                            exps(c, uc, j)

                def q_groups(*groups):
                    a, v = n + 1, (u + 1) % 4
                    if there(a, BLOCKS):
                        for g in groups:
                            wait(act, s_qin[v // 2], 16 * Q_DMAS * (a // 4 + 1))
                            wait(act, s_stp, STU * (a - 3))
                            at = (v % 2) * P + g * GQ
                            act.copy(qs[0:KROWS, v, g], qin[:, v // 2, :, at:at + GQ]).then_inc(s_qs, 1)

                q_groups(0, 1)
                if there(m, BLOCKS):
                    wait(act, s_mtp, m + 1)
                    wait(act, s_m[(u - 3) % 4], 16 * ((m - 2) // 4 + 1))
                    act.copy(mt[:, (u - 1) % 2], trbank[0:PARTS * 16, 0:P // 2].bitcast(BF16)).then_inc(s_mt, 1)
                if there(e, BLOCKS):
                    wait(act, s_xtp, e + 1)
                    wait(act, s_ffn, e)
                    act.copy(x2nT[:].rearrange("p c t -> p (c t)"), xtbank[:, 0:WIDTH]).then_inc(s_x2nT, 1)
                ex(0)
                q_groups(2)
                ex(1)
                q_groups(3)
                ex(2)
                if there(b, BLOCKS):
                    wait(act, s_ntp, b + 1)
                    wait(act, s_wf, b)
                    act.copy(onT[:].rearrange("p c t -> p (c t)"), trbank[:, 0:WIDTH]).then_inc(s_onT, 1)
                ex(3, 4)

            p2_loop(act, p2)

        @block.vector
        def _(dve):
            dve.memset(zero[:], 0.0).then_inc(s_zero, 1)
            dve.memset(neghalf[:], -0.5)
            dve.memset(bdmask[:], 0.0)
            dve.memset(vn[:], 0.0)
            dve.memset(mp[:], 0.0)
            dve.memset(qs[KROWS:KALL], 1.0).then_inc(s_set, 1)
            dve.wait_ge(s_set, 1)
            dve.memset(vn[:, :, :, HD:HD + 1], 1.0)
            for g in range(GROUPS):
                last = dve.memset(bdmask[g * GQ:(g + 1) * GQ, g], 1.0)
            last.then_inc(s_set, 1)
            def p1(s, par):
                ln, pj, vt = s + 2, s, s - 1
                if there(ln, TILES):
                    wait(dve, s_x1[par], 16 * (ln // 2 + 1))
                    wait(dve, s_mv1, TJ * ln)
                    for j in range(TJ):
                        dve.bn_stats(st1[:, j], xt[:, par, j]).then_inc(s_st1, 1)
                    wait(dve, s_st1, TJ * (ln + 1))
                    wait(dve, s_xn, ln)
                    dve.memset(tick[:], 0.0)
                    for j in range(TJ):
                        dve.bn_aggr(mv1[:, j], st1[:, j]).then_inc(s_mv1, 1)
                    wait(dve, s_mv1, TJ * (ln + 1))
                    wait(dve, s_rs1, ln)
                    dve.tensor_scalar(ve1[:], mv1[:, :, 1], EPS, None, ALU.add).then_inc(s_ve1, 1)
                def remainder(h):
                    if there(pj, TILES):
                        wait(dve, s_q1, FC * pj + h + 1)
                        wait(dve, s_q3, FC * (pj - 1) + h + 1)
                        dve.tensor_tensor(qr[:, h], qbank[:, h], qp[:, par, 0, h], ALU.subtract
                                          ).then_inc(s_qr, 1)

                remainder(0)
                if there(vt, TILES):
                    wait(dve, s_vt, vt + 1)
                    wait(dve, s_stv[1 - par], 16 * (vt // 2))
                    dve.tensor_copy(vn[:, 1 - par, :, 0:HD],
                                    bank[3][:, 0:P].rearrange("p (j c) -> p j c", c=KV)[:, :, HD:KV]
                                    ).then_inc(s_vn, 1)
                if there(ln, TILES):
                    wait(dve, s_rs1, ln + 1)
                    wait(dve, s_tr1, FC * (ln - 1))
                    for j in range(TJ):
                        last = dve.tensor_scalar(xn[:, par, j], xt[:, par, j], mv1[:, j, 0:1], rs1[:, j:j + 1],
                                                 ALU.subtract, ALU.mult)
                    last.then_inc(s_xn, 1)
                remainder(1)

            p1_loop(dve, p1)

            dve.wait_ge(s_const, 16 * (len(consts) - EARLY))
            dve.wait_ge(s_low, 3)
            dve.tensor_tensor(weff[:].rearrange("p c n -> p (c n)"), bank[4][:, :],
                              wffn[:].rearrange("p c n -> p (c n)"), ALU.add).then_inc(s_weff, 1)

            def p2(n, u):
                m, b, e = n - 1, n - 3, n - 4
                par = u % 2

                def mx_(*units):
                    if there(n, BLOCKS):
                        for j in units:
                            wait(dve, s_sc, UNITS * n + j + 1)
                            dve.tensor_reduce(mx[:, par, 2 * j:2 * j + 2],
                                              sbank[j % 2][:, 0:2 * GWIN].rearrange("p (k c) -> p k c", k=2),
                                              AX.X, ALU.max).then_inc(s_mx, 1)

                m_ = mx[:, (u - 1) % 2]
                if there(e, BLOCKS):
                    wait(dve, s_st2, e + 1)
                    dve.memset(tick[:], 0.0)
                    dve.bn_aggr(mv2[:], st2[:]).then_inc(s_mv2, 1)
                if there(m, BLOCKS):
                    wait(dve, s_mx, UNITS * (m + 1))
                    wait(dve, s_mtp, m)
                    dve.tensor_copy(mp[:, 0], m_).then_inc(s_mp1, 1)
                if there(e, BLOCKS):
                    wait(dve, s_mv2, e + 1)
                    dve.tensor_scalar(ve2[:], mv2[:, 1:2], EPS, None, ALU.add).then_inc(s_ve2, 1)
                if there(m, BLOCKS):
                    wait(dve, s_mp1, m + 1)
                    dve.tensor_tensor(mr[:, 0], m_, mp[:, 0], ALU.subtract).then_inc(s_mr1, 1)
                    wait(dve, s_mr1, m + 1)
                    dve.tensor_copy(mp[:, 1], mr[:, 0]).then_inc(s_mp2, 1)
                mx_(0)
                if there(m, BLOCKS):
                    wait(dve, s_mp2, m + 1)
                    dve.tensor_tensor(mp[:, 2], mr[:, 0], mp[:, 1], ALU.subtract).then_inc(s_mp, 1)
                if there(e, BLOCKS):
                    wait(dve, s_rs2, e + 1)
                    wait(dve, s_xtp, e)
                    dve.tensor_scalar(x2n[:], x2[:], mv2[:, 0:1], rs2[:], ALU.subtract, ALU.mult
                                      ).then_inc(s_x2n, 1)
                if there(b, BLOCKS):
                    wait(dve, s_pv, b + 1)
                    wait(dve, s_on, b)
                    dve.transpose(ot[:].rearrange("p h c -> p (h c)"), pvbank[:, :]).then_inc(s_ot, 1)
                mx_(1)
                if there(b, BLOCKS):
                    wait(dve, s_ot, b + 1)
                    dve.reciprocal(rden[:], ot[:, :, HD]).then_inc(s_rd, 1)
                mx_(2)
                if there(b, BLOCKS):
                    wait(dve, s_rd, b + 1)
                    wait(dve, s_ntp, b)
                    dve.tensor_tensor(on[:].rearrange("p (h d) -> p h d", d=HD), ot[:, :, 0:HD],
                                      rden[:].unsqueeze(2).to_broadcast([P, HEADS, HD]), ALU.mult
                                      ).then_inc(s_on, 1)
                mx_(3)
                if there(e, BLOCKS):
                    wait(dve, s_ffn, e + 1)
                    wait(dve, s_x2b, e + 1)
                    wait(dve, s_out[u % 4 // 2], 16 * (e // 4))
                    dve.tensor_tensor(ob[:, u], dbank[:, 0:WIDTH], x2b[:], ALU.add).then_inc(s_ob, 1)
                mx_(4, 5, 6)
                if there(b, BLOCKS):
                    wait(dve, s_wf, b + 1)
                    wait(dve, s_xb, b + 1)
                    wait(dve, s_x2b, b)
                    dve.tensor_tensor(x2[:], dbank[:, 0:WIDTH], xr[:, (u - 3) % 4], ALU.add).then_inc(s_x2, 1)
                if there(b, BLOCKS):
                    wait(dve, s_x2, b + 1)
                    dve.bn_stats(st2[:], x2[:]).then_inc(s_st2, 1)
                mx_(7)

            p2_loop(dve, p2)

        @block.gpsimd
        def _(pool):
            pool.wait_ge(s_set, 2)

            def p1(s, par):
                ln, pj = s + 2, s
                if there(ln, TILES):
                    wait(pool, s_ve1, ln + 1)
                    wait(pool, s_xn, ln)
                    pool.tensor_tensor(rs1[:], ve1[:], neghalf[:], ALU.pow).then_inc(s_rs1, 1)
                if there(pj, TILES):
                    wait(pool, s_k1, pj + 1)
                    wait(pool, s_k3, pj)
                    pool.tensor_tensor(kr[:], kvS[:], kp[:, par, 2], ALU.subtract).then_inc(s_kr, 1)
                    wait(pool, s_k2, pj + 1)
                    pool.tensor_tensor(kp[:, par, 0], kr[:], kp[:, par, 1], ALU.subtract).then_inc(s_k3, 1)
                    for h in range(FC):
                        wait(pool, s_q2, FC * pj + h + 1)
                        pool.tensor_tensor(qp[:, par, 2, h], qr[:, h], qp[:, par, 1, h], ALU.subtract
                                           ).then_inc(s_q3, 1)

            p1_loop(pool, p1)
            pool.wait_ge(s_const, 16 * (len(consts) - EARLY))

            def p2(n, u):
                c, e = n - 2, n - 4
                uc = (u - 2) % 4

                def select(g):
                    wait(pool, s_ex, STU * c + g + 1)
                    pool.tensor_tensor(ptick[:, g:g + 1], neghalf[0:1, 0:1], neghalf[0:1, 0:1], ALU.add)
                    v = pm[0:GQ, uc % 2, g].rearrange("p (h q) -> p h q", h=HEADS)
                    pool.affine_select(out=v, in_=v, compare_op=ALU.is_ge, fill=0.0, base=0,
                                       pattern=[[0, HEADS], [-1, GQ]], channel_multiplier=1).then_inc(s_sel, 1)

                if there(e, BLOCKS):
                    wait(pool, s_ve2, e + 1)
                    wait(pool, s_x2n, e)
                    pool.tensor_tensor(rs2[:], ve2[:], neghalf[:, 0:1], ALU.pow).then_inc(s_rs2, 1)
                    wait(pool, s_x2, e + 1)
                    wait(pool, s_ob, e)
                    pool.tensor_tensor(x2b[:], x2[:], b_bc[:], ALU.add).then_inc(s_x2b, 1)
                if there(c, BLOCKS):
                    wait(pool, s_v[uc], 16 * (c // 4 + 1))
                    wait(pool, s_pv, c - 1)
                    pool.tensor_tensor(vbd[:, uc % 2], vm[:, uc, GROUPS].unsqueeze(1).to_broadcast([P, GROUPS, VW]),
                                       bdmask[:], ALU.mult).then_inc(s_vbd, 1)
                    wait(pool, s_xin[uc // 2], 16 * (c // 4 + 1))
                    pool.tensor_tensor(xr[:, uc], xr[:, uc], bf_bc[:], ALU.add).then_inc(s_xb, 1)
                    for g in range(GROUPS):
                        select(g)

            p2_loop(pool, p2)


def kernel(L0_attn_x, L0_attn_Wq, L0_attn_Wk, L0_attn_Wv, L0_attn_Wf, L0_attn_bf, L0_ffn_W, L0_ffn_b,
           L0_ffn_lora_down, L0_ffn_lora_up, L0_ffn_down_aux, L0_ffn_up_aux):
    import ml_dtypes
    import numpy as np
    import concourse.bacc as bacc
    from concourse.bass_utils import run_bass_kernel_spmd

    bf = ml_dtypes.bfloat16
    f = np.float32
    wkv = np.concatenate([np.asarray(L0_attn_Wk), np.asarray(L0_attn_Wv)], axis=0).T
    edge = np.zeros((1 + PARTS, BATCH, LP), f)
    edge[0, :, 0:WINDOW] = NEG
    edge[0, :, WINDOW + SEQ:] = NEG
    edge[1:] = -1.0
    i = np.arange(GQ)
    onehot = np.tile(np.eye(GQ, dtype=f), (1, P // GQ))
    corner = np.zeros((GQ, 2, 2, GQ), f)
    corner[:, :, 0] = np.where(i[None, :] < i[:, None], NEG, 0.0)[:, None, :]
    corner[:, :, 1] = np.where(i[None, :] > i[:, None], NEG, 0.0)[:, None, :]
    rem = np.tile(np.where(i[None, :] > i[:, None], NEG, 0.0), (1, GROUPS))
    data = {
        "x": np.asarray(L0_attn_x).reshape(TOKENS, WIDTH),
        "wq_t": np.asarray(L0_attn_Wq).T, "wkv_t": wkv, "wf_t": np.asarray(L0_attn_Wf).T,
        "bf_rows": np.broadcast_to(np.asarray(L0_attn_bf), (P, WIDTH)),
        "wffn_t": np.asarray(L0_ffn_W).T, "b_rows": np.broadcast_to(np.asarray(L0_ffn_b), (P, WIDTH)),
        "down_t": np.asarray(L0_ffn_lora_down).T, "up_t": np.asarray(L0_ffn_lora_up).T,
        "down_aux": np.asarray(L0_ffn_down_aux), "up_aux_t": np.asarray(L0_ffn_up_aux).T,
        "edge_rows": edge.reshape(1 + PARTS, BATCH * LP).astype(bf),
        "onehot": onehot.astype(bf), "corners": corner.astype(bf), "rem_mask": rem.astype(bf),
        "onehot_cols": np.tile(np.eye(GQ, dtype=f), (1, HEADS)).astype(bf),
        "ident": np.eye(P, dtype=f), "ident_b": np.eye(P, dtype=f).astype(bf),
    }
    nc = bacc.Bacc("TRN2", target_bir_lowering=False, num_devices=1)
    arrays, args = {}, []
    for name, a in data.items():
        arrays[f"in_{name}"] = a = np.ascontiguousarray(a)
        args.append(nc.dram_tensor(f"in_{name}", a.shape, mybir.dt.from_np(a.dtype), kind="ExternalInput").ap())
    args.append(nc.dram_tensor("out_y", (TOKENS, WIDTH), F32, kind="ExternalOutput").ap())
    build(nc, *args)
    r = run_bass_kernel_spmd(nc, [arrays], core_ids=[0])
    return r.results[0]["out_y"].reshape(BATCH, SEQ, WIDTH)
```

```python
from contextlib import ExitStack

import concourse.bass as bass
from concourse import mybir

F32 = mybir.dt.float32
BF16 = mybir.dt.bfloat16
ALU = mybir.AluOpType
ACT = mybir.ActivationFunctionType
AX = mybir.AxisListType

P = 128
BATCH, SEQ, WIDTH = 4, 2048, 256
HEADS, HD = 16, 16
WINDOW = 64
TOKENS = BATCH * SEQ
TILE = 512
TILES = TOKENS // TILE
TJ = TILE // P
BLOCKS = TOKENS // P
BPS = SEQ // P
GQ = 32
GROUPS = P // GQ
GWIN = GQ + 2 * WINDOW
KWIN = P + 2 * WINDOW
LP = SEQ + 2 * WINDOW
VW = 32
KV = 2 * HD
PARTS = 3
KROWS = 6 * HD
KEDGE = KROWS + 1
KALL = KEDGE + PARTS
KSTORE = PARTS * HD + KALL - KROWS
FC = WIDTH // P
RING = 4
UNITS = 2 * GROUPS
STU = GROUPS + 1
NEG = -1.0e30
EPS = 1e-5
SCALE = HD ** -0.5
DDIM, UDIM, RANK = 100, 50, 4

S_DMAS = 1 + TJ
K_DMAS = 3
Q_DMAS = 6


def wait(engine, semaphore, value):
    if isinstance(value, int) and value <= 0:
        return
    engine.wait_ge(semaphore, value)


def there(i, n):
    return not isinstance(i, int) or 0 <= i < n


def seen(count):
    return min(count, BLOCKS) if isinstance(count, int) else count


def build(nc, x, wq_t, wkv_t, wf_t, bf_rows, wffn_t, b_rows, down_t, up_t, down_aux, up_aux_t,
          edge_rows, onehot, corners, rem_mask, onehot_cols, ident, ident_b,
          ones_row, out):
    q_scr = nc.dram_tensor("q_scratch", (PARTS, WIDTH, TOKENS), BF16, kind="Internal").ap()
    k_scr = nc.dram_tensor("k_scratch", (KSTORE, BATCH * LP), BF16, kind="Internal").ap()
    v_scr = nc.dram_tensor("v_scratch", (BATCH * LP, VW), F32, kind="Internal").ap()

    ctx = ExitStack()
    with ctx:
        def sb(name, shape, dt=F32):
            return ctx.enter_context(nc.sbuf_tensor(name, shape, dt))

        def sem(name):
            return ctx.enter_context(nc.semaphore(name))

        wq = sb("wq", [P, FC, WIDTH])
        wkv = sb("wkv", [P, FC, KV])
        wf = sb("wf", [P, FC, WIDTH])
        bf_bc = sb("bf_bc", [P, WIDTH])
        b_bc = sb("b_bc", [P, WIDTH])
        wffn = sb("wffn", [P, FC, WIDTH])
        weff = sb("weff", [P, FC, WIDTH])
        downT = sb("downT", [DDIM, RANK])
        upT = sb("upT", [RANK, UDIM])
        daux = sb("daux", [DDIM, WIDTH])
        uauxT = sb("uauxT", [UDIM, WIDTH])
        low1 = sb("low1", [RANK, WIDTH])
        low2 = sb("low2", [UDIM, WIDTH])
        hot = sb("hot", [GQ, P], BF16)
        corner = sb("corner", [GQ, 2, 2, GQ], BF16)
        remm = sb("remm", [GQ, P], BF16)
        hotc = sb("hotc", [GQ, HEADS * GQ], BF16)
        idf = sb("idf", [P, P])
        idb = sb("idb", [P, P], BF16)
        tick = sb("tick", [1, 1])
        ptick = sb("ptick", [1, GROUPS])
        neghalf = sb("neghalf", [P, TJ])
        bdmask = sb("bdmask", [P, GROUPS, VW])
        zero = sb("zero", [P, P])

        xt = sb("xt", [P, 2, TJ, WIDTH])
        st1 = sb("st1", [P, TJ, 6])
        mv1 = sb("mv1", [P, TJ, 2])
        ve1 = sb("ve1", [P, TJ])
        rs1 = sb("rs1", [P, TJ])
        xn = sb("xn", [P, 2, TJ, WIDTH])
        xnT = sb("xnT", [P, 2, FC, TILE])
        qp = sb("qp", [P, 2, PARTS, FC, TILE], BF16)
        qr = sb("qr", [P, FC, TILE])
        kvS = sb("kvS", [P, P])
        kp = sb("kp", [P, 2, PARTS, P], BF16)
        kr = sb("kr", [P, P])
        vn = sb("vn", [P, 2, TJ, VW])

        qin = sb("qin", [KROWS, 2, HEADS, 2 * P], BF16)
        qs = sb("qs", [KALL, RING, GROUPS, HEADS, GQ], BF16)
        ks = sb("ks", [KALL, RING, KWIN], BF16)
        vm = sb("vm", [P, RING, GROUPS + 1, VW])
        vbd = sb("vbd", [P, 2, GROUPS, VW])
        xr = sb("xr", [P, RING, WIDTH])
        mx = sb("mx", [P, 2, 16])
        mp = sb("mp", [P, P // 16, 16], BF16)
        mr = sb("mr", [P, 2, 16])
        mt = sb("mt", [PARTS * 16, 2, P], BF16)
        pm = sb("pm", [P, 2, GROUPS, HEADS * GQ])
        pr = sb("pr", [P, 2, HEADS * GQ])
        ot = sb("ot", [P, HEADS, VW])
        rden = sb("rden", [P, HEADS])
        on = sb("on", [P, WIDTH])
        onT = sb("onT", [P, FC, P])
        x2 = sb("x2", [P, WIDTH])
        st2 = sb("st2", [P, 6])
        mv2 = sb("mv2", [P, 2])
        ve2 = sb("ve2", [P, 1])
        rs2 = sb("rs2", [P, 1])
        x2n = sb("x2n", [P, WIDTH])
        x2nT = sb("x2nT", [P, FC, P])
        x2b = sb("x2b", [P, WIDTH])
        ob = sb("ob", [P, 4, WIDTH])

        bank = [ctx.enter_context(nc.psum_tensor(f"bank{i}", [P, 512], F32)) for i in range(5)]
        qbank = ctx.enter_context(nc.psum_tensor("qbank", [P, FC, 512], F32))
        b7 = ctx.enter_context(nc.psum_tensor("bank7", [P, 512], F32))
        sbank, tbank, pvbank, xtbank, trbank, dbank = bank[0:2], bank[2:4], bank[4], qbank[:, 0], qbank[:, 1], b7

        s_early = sem("s_early")
        s_const = sem("s_const")
        s_set = sem("s_set")
        s_zero = sem("s_zero")
        s_halo = sem("s_halo")
        s_low = sem("s_low")
        s_lowc = sem("s_lowc")
        s_weff = sem("s_weff")

        s_x1 = [sem(f"s_x1_{i}") for i in range(2)]
        s_st1, s_mv1, s_ve1, s_rs1, s_xn = (sem(n) for n in ("s_st1", "s_mv1", "s_ve1", "s_rs1", "s_xn"))
        s_tr1, s_xnT, s_q, s_kv, s_vt = (sem(n) for n in ("s_tr1", "s_xnT", "s_q", "s_kv", "s_vt"))
        s_q1, s_qr, s_q2, s_q3 = (sem(n) for n in ("s_q1", "s_qr", "s_q2", "s_q3"))
        s_kvs, s_k1, s_kr, s_k2, s_k3, s_vn = (sem(n) for n in ("s_kvs", "s_k1", "s_kr", "s_k2", "s_k3", "s_vn"))
        s_stq = [sem(f"s_stq{i}") for i in range(2)]
        s_stv = [sem(f"s_stv{i}") for i in range(2)]

        s_qin = [sem(f"s_qin{i}") for i in range(2)]
        s_qs = sem("s_qs")
        s_k = [sem(f"s_k_{i}") for i in range(RING)]
        s_v = [sem(f"s_v{i}") for i in range(RING)]
        s_xin = [sem(f"s_xin{i}") for i in range(RING // 2)]
        s_m = [sem(f"s_m{i}") for i in range(RING)]
        s_out = [sem(f"s_out{i}") for i in range(2)]
        s_sc, s_mx, s_mp1, s_mr1, s_mp2, s_mp = (sem(n) for n in (
            "s_sc", "s_mx", "s_mp1", "s_mr1", "s_mp2", "s_mp"))
        s_mtp, s_mt = sem("s_mtp"), sem("s_mt")
        s_stp, s_ex, s_sel, s_vbd = (sem(n) for n in ("s_stp", "s_ex", "s_sel", "s_vbd"))
        s_pv, s_ot, s_rd, s_on = (sem(n) for n in ("s_pv", "s_ot", "s_rd", "s_on"))
        s_ntp, s_onT, s_wf, s_xb, s_x2, s_st2, s_mv2, s_ve2, s_rs2 = (sem(n) for n in (
            "s_ntp", "s_onT", "s_wf", "s_xb", "s_x2", "s_st2", "s_mv2", "s_ve2", "s_rs2"))
        s_x2n, s_xtp, s_x2nT, s_ffn, s_x2b, s_ob = (sem(n) for n in (
            "s_x2n", "s_xtp", "s_x2nT", "s_ffn", "s_x2b", "s_ob"))

        consts = [
            (idf[:], ident), (wkv[:], wkv_t.rearrange("(c p) n -> p c n", p=P)),
            (wq[:], wq_t.rearrange("(c p) n -> p c n", p=P)),
            (wf[:], wf_t.rearrange("(c p) n -> p c n", p=P)), (wffn[:], wffn_t.rearrange("(c p) n -> p c n", p=P)),
            (bf_bc[:], bf_rows), (b_bc[:], b_rows), (downT[:], down_t), (upT[:], up_t), (daux[:], down_aux),
            (uauxT[:], up_aux_t), (hot[:], onehot), (corner[:], corners), (remm[:], rem_mask),
            (hotc[:], onehot_cols), (idb[:], ident_b),
            (qs[KROWS:KEDGE].rearrange("o r g h q -> o (r g h q)"), ones_row),
        ]
        EARLY = 3

        block = ctx.enter_context(nc.Block())

        def p1_loop(engine, step, setup):
            for s in range(-2, 4):
                step(s, s % 2)
                if 0 <= s < 3:
                    setup(s)
            with engine.Fori(2, TILES // 2 - 2) as i:
                for u in range(2):
                    step(2 * i + u, u)
            for s in range(TILES - 4, TILES - 2):
                step(s, s % 2)

        def between(p1, p2, hand_over=lambda n: None):
            p1(TILES - 2, 0)
            hand_over(-1)
            p1(TILES - 1, 1)
            hand_over(0)
            p2(0, 0)
            hand_over(1)
            p1(TILES, 0)
            p2(1, 1)
            hand_over(2)

        def p2_loop(engine, step):
            for n in range(2, 8):
                step(n, n % 4)
            with engine.Fori(2, BLOCKS // 4 - 1) as t:
                for u in range(4):
                    step(4 * t + u, u)
            for n in range(BLOCKS - 4, BLOCKS + 5):
                step(n, n % 4)

        @block.sync
        def _(sp):
            def load_x(ld, par):
                sp.dma_start(xt[:, par], x[bass.ds(ld * TILE, TILE), :].rearrange("(j p) f -> p j f", p=P)
                             ).then_inc(s_x1[par], 16)

            load_x(0, 0)
            for dst, src in consts[:EARLY]:
                sp.dma_start(dst, src).then_inc(s_early, 16)
            load_x(1, 1)
            for dst, src in consts[EARLY:]:
                sp.dma_start(dst, src).then_inc(s_const, 16)

            def halos():
                sp.wait_ge(s_zero, 1)
                sp.dma_start(k_scr[PARTS * HD:KSTORE, :], edge_rows).then_inc(s_halo, 16)
                for at in (0, WINDOW + SEQ):
                    sp.dma_start(k_scr[0:PARTS * HD, :].rearrange("r (b l) -> r b l", b=BATCH)[:, :, at:at + WINDOW],
                                 zero[0:PARTS * HD, 0:BATCH * WINDOW // 2].bitcast(BF16)).then_inc(s_halo, 16)
                    sp.dma_start(v_scr.rearrange("(b l) c -> l b c", b=BATCH)[at:at + WINDOW],
                                 zero[0:WINDOW, 0:BATCH * VW]).then_inc(s_halo, 16)

            def p1(s, par):
                ld, pj, vt = s + 4, s, s - 1
                if there(ld, TILES):
                    wait(sp, s_xn, ld - 1)
                    load_x(ld, par)
                if there(pj, TILES):
                    wait(sp, s_q3, FC * (pj + 1))
                    sp.dma_start(q_scr[:, :, bass.ds(pj * TILE, TILE)].rearrange("a (c p) t -> p (a c) t", p=P),
                                 qp[:, par].rearrange("p a c t -> p (a c) t")).then_inc(s_stq[par], 16)
                    wait(sp, s_k3, pj + 1)
                    at = pj * TILE + (pj * TILE // SEQ) * (LP - SEQ) + WINDOW
                    for j in range(TJ):
                        sp.dma_start(k_scr[0:PARTS * HD, bass.ds(at + j * P, P)].rearrange("(a d) t -> d a t", d=HD),
                                     kp[j * KV:j * KV + HD, par]).then_inc(s_stq[par], 16)
                if there(vt, TILES):
                    wait(sp, s_vn, vt + 1)
                    at = vt * TILE + (vt * TILE // SEQ) * (LP - SEQ) + WINDOW
                    sp.dma_start(v_scr[bass.ds(at, TILE), :].rearrange("(j p) c -> p j c", p=P),
                                 vn[:, 1 - par]).then_inc(s_stv[1 - par], 16)

            def q_load(a, u):
                if there(a, BLOCKS):
                    wait(sp, s_qs, GROUPS * (a - 2))
                    row = 0
                    for part, copies in ((0, 3), (1, 2), (2, 1)):
                        for _ in range(copies):
                            sp.dma_start(qin[row:row + HD, u // 2],
                                         q_scr[part, :, bass.ds(a * P, 2 * P)].rearrange("(h d) t -> d h t", d=HD)
                                         ).then_inc(s_qin[u // 2], 16)
                            row += HD

            def loads(n, u):
                a, vb, xb_ = n, n - 1, n - 2
                if u % 2 == 1:
                    q_load(n + 1, (u + 1) % 4)
                if there(a, BLOCKS):
                    wait(sp, s_stp, STU * (a - 3))
                    sl = u
                    at = a * P + (a // BPS) * (LP - SEQ)
                    for row, k_row, rows in ((0, 0, 3 * HD), (3 * HD, HD, 2 * HD), (5 * HD, 2 * HD, KSTORE - 2 * HD)):
                        sp.dma_start(ks[row:row + rows, sl], k_scr[k_row:k_row + rows, bass.ds(at, KWIN)]
                                     ).then_inc(s_k[sl], 16)
                if there(vb, BLOCKS):
                    sl = (u - 1) % 4
                    wait(sp, s_pv, vb - 3)
                    at = vb * P + (vb // BPS) * (LP - SEQ)
                    row = v_scr[bass.ds(at, P), :]
                    sp.dma_start(vm[:, sl], bass.AP(row.tensor, row.offset, [[VW, P], [GQ * VW, GROUPS + 1], [1, VW]])
                                 ).then_inc(s_v[sl], 16)
                if u % 2 == 0 and there(xb_, BLOCKS):
                    sl = (u - 2) % 4
                    wait(sp, s_x2, xb_ - 2)
                    sp.dma_start(xr[:, sl:sl + 2], x[bass.ds(xb_ * P, 2 * P), :].rearrange(
                        "(i p) f -> p i f", p=P)).then_inc(s_xin[sl // 2], 16)

            def stores(n, u):
                m, e = n - 2, n - 5
                if there(m, BLOCKS):
                    sl = (u - 2) % 4
                    wait(sp, s_mt, m + 1)
                    sp.dma_start(qs[KEDGE:KALL, sl].rearrange("o g h q -> o (g h q)"), mt[:, u % 2]
                                 ).then_inc(s_m[sl], 16)
                if u % 2 == 0 and there(e, BLOCKS):
                    sl = (u - 6) % 4
                    wait(sp, s_ob, e + 1)
                    sp.dma_start(out[bass.ds((e - 1) * P, 2 * P), :].rearrange("(i p) f -> p i f", p=P),
                                 ob[:, sl:sl + 2]).then_inc(s_out[sl // 2], 16)

            for s in range(-2, 4):
                p1(s, s % 2)
                if s == -2:
                    halos()
            with sp.Fori(2, TILES // 2 - 2) as i:
                for u in range(2):
                    p1(2 * i + u, u)
            sp.wait_ge(s_halo, 16 * 5)
            for par in range(2):
                sp.wait_ge(s_stq[par], 16 * S_DMAS)
                sp.wait_ge(s_stv[par], 16)
            q_load(0, 0)
            for n in range(-1, 3):
                p1(TILES - 3 + n, (n + 1) % 2)
                if n < 2:
                    loads(n + 1, n + 1)
            p1(TILES, 0)
            stores(2, 2)
            for n in range(3, 8):
                if n == 6:
                    for par in range(2):
                        sp.wait_ge(s_stq[par], S_DMAS * 16 * TILES // 2)
                        sp.wait_ge(s_stv[par], 16 * TILES // 2)
                loads(n, n % 4)
                stores(n, n % 4)
            with sp.Fori(2, BLOCKS // 4 - 1) as t:
                for u in range(4):
                    loads(4 * t + u, u)
                    stores(4 * t + u, u)
            for n in range(BLOCKS - 4, BLOCKS + 5):
                loads(n, n % 4)
                stores(n, n % 4)
            for par in range(2):
                sp.wait_ge(s_out[par], 16 * BLOCKS // 4)

        @block.tensor
        def _(pe):
            pe.wait_ge(s_early, 16 * EARLY)

            def p1(s, par):
                tr, pj, vt = s + 1, s, s - 1
                def q(h):
                    if there(pj, TILES):
                        wait(pe, s_qr, FC * (pj - 1) + h + 1)
                        for c in range(FC):
                            mm = pe.matmul(qbank[:, h], wq[:, c, h * P:(h + 1) * P], xnT[:, par, c],
                                           start=(c == 0), stop=(c == FC - 1))
                        mm.then_inc(s_q, 1)

                if there(vt, TILES):
                    wait(pe, s_kvs, vt + 1)
                    wait(pe, s_vn, vt)
                    pe.transpose(bank[3][:, 0:P], kvS[:], idf[:]).then_inc(s_vt, 1)
                if there(pj, TILES):
                    wait(pe, s_xnT, (pj + 1) * FC)
                    wait(pe, s_kvs, pj)
                    for c in range(FC):
                        for j in range(TJ):
                            mm = pe.matmul(bank[2][j * KV:(j + 1) * KV, 0:P], wkv[:, c],
                                           xnT[:, par, c, j * P:(j + 1) * P], start=(c == 0), stop=(c == FC - 1),
                                           skip_group_check=True)
                    mm.then_inc(s_kv, 1)
                q(0)
                if there(tr, TILES):
                    wait(pe, s_xn, tr + 1)
                    wait(pe, s_xnT, tr * FC)
                    for c in range(FC):
                        for j in range(TJ):
                            mm = pe.transpose(bank[c][:, j * P:(j + 1) * P],
                                              xn[:, 1 - par, j, c * P:(c + 1) * P], idf[:])
                        mm.then_inc(s_tr1, 1)
                q(1)

            def setup(k):
                if k == 0:
                    pe.wait_ge(s_const, 16 * (len(consts) - EARLY))
                    pe.matmul(bank[4][0:RANK, 0:WIDTH], downT[:], daux[:], start=True, stop=True
                              ).then_inc(s_low, 1)
                elif k == 1:
                    pe.wait_ge(s_lowc, 1)
                    pe.matmul(bank[4][0:UDIM, 0:WIDTH], upT[:], low1[:], start=True, stop=True).then_inc(s_low, 1)
                else:
                    pe.wait_ge(s_lowc, 2)
                    for c in range(FC):
                        mm = pe.matmul(bank[4][:, c * WIDTH:(c + 1) * WIDTH], low2[:, c * P:(c + 1) * P], uauxT[:],
                                       start=True, stop=True)
                    mm.then_inc(s_low, 1)

            p1_loop(pe, p1, setup)

            def hand_over(n):
                if n == 0:
                    pe.wait_ge(s_xnT, FC * TILES)
                elif n == 1:
                    pe.wait_ge(s_qr, FC * TILES)
                elif n == 2:
                    pe.wait_ge(s_vn, TILES)
                    pe.wait_ge(s_weff, 1)

            def scores(n, u, j):
                g, hp = j // 2, j % 2
                tile = sbank[j % 2]
                wait(pe, s_mx, UNITS * n + j - 1)
                for k in range(2):
                    h = 8 * hp + 4 * k
                    pe.matmul(tile[:, k * GWIN:(k + 1) * GWIN], qs[0:KEDGE, u, g, h:h + 4],
                              ks[0:KEDGE, u, g * GQ:g * GQ + GWIN], start=(k == 0), stop=False,
                              skip_group_check=True)
                dst = tile[:, 0:2 * GWIN].rearrange("p (k s c) -> p k s c", k=2, c=GQ)[:, :, 0:5:4, :]
                pe.matmul(dst, hot[:], corner[:], start=False, stop=True, skip_group_check=True).then_inc(s_sc, 1)

            def scores_t(n, u, j):
                tile = tbank[(STU * u + j) % 2]
                if j == 0:
                    wait(pe, s_m[u], 16 * (n // 4 + 1))
                wait(pe, s_ex, STU * n + j - 1)
                if j < GROUPS:
                    pe.matmul(tile[:, :], ks[0:KALL, u, j * GQ:j * GQ + P], qs[0:KALL, u, j],
                              start=True, stop=True).then_inc(s_stp, 1)
                else:
                    for g in range(GROUPS):
                        at = P + g * GQ
                        pe.matmul(tile[g * GQ:(g + 1) * GQ, :], ks[0:KALL, u, at:at + GQ],
                                  qs[0:KALL, u, g], start=True, stop=False,
                                  skip_group_check=True)
                    pe.matmul(tile[:, :], remm[:], hotc[:], start=False, stop=True,
                              skip_group_check=True).then_inc(s_stp, 1)

            def times_v(n, u, last):
                par = u % 2
                if last:
                    wait(pe, s_ex, STU * (n + 1))
                    wait(pe, s_vbd, n + 1)
                    pe.matmul(pvbank[:, :], vbd[:, par].rearrange("p g c -> p (g c)"), pr[:, par],
                              start=False, stop=True, skip_group_check=True).then_inc(s_pv, 1)
                else:
                    wait(pe, s_ot, n)
                    wait(pe, s_v[u], 16 * (n // 4 + 1))
                    for g in range(GROUPS):
                        wait(pe, s_sel, GROUPS * n + g + 1)
                        pe.matmul(pvbank[g * VW:(g + 1) * VW, :], vm[:, u, g], pm[:, par, g],
                                  start=True, stop=False, skip_group_check=True)

            def p2(n, u):
                m, c, b, e = n - 1, n - 2, n - 3, n - 4
                um, uc, ub, ue = ((u - k) % 4 for k in (1, 2, 3, 4))

                def s(*units):
                    if there(n, BLOCKS):
                        for j in units:
                            scores(n, u, j)

                def st(j):
                    if there(c, BLOCKS):
                        scores_t(c, uc, j)

                if there(n, BLOCKS):
                    wait(pe, s_qs, GROUPS * (n + 1))
                    wait(pe, s_k[u], 16 * K_DMAS * (n // 4 + 1))
                s(0)
                if there(b, BLOCKS):
                    times_v(b, ub, 0)
                s(1)
                if there(b, BLOCKS):
                    times_v(b, ub, 1)
                if there(m, BLOCKS):
                    wait(pe, s_mp, m + 1)
                    wait(pe, s_onT, m - 2)
                    wait(pe, s_mt, m)
                    pe.transpose(trbank[:, 0:P // 2].bitcast(BF16), mp[:].rearrange("p a c -> p (a c)"),
                                 idb[:]).then_inc(s_mtp, 1)
                s(2)
                if there(e, BLOCKS):
                    wait(pe, s_x2n, e + 1)
                    wait(pe, s_x2nT, e)
                    for k in range(FC):
                        mm = pe.transpose(xtbank[:, k * P:(k + 1) * P], x2n[:, k * P:(k + 1) * P], idf[:])
                    mm.then_inc(s_xtp, 1)
                st(0)
                st(1)
                s(3)
                if there(e, BLOCKS):
                    wait(pe, s_x2nT, e + 1)
                    wait(pe, s_x2, e + 1)
                    for k in range(FC):
                        mm = pe.matmul(dbank[:, 0:WIDTH], x2nT[:, k], weff[:, k], start=(k == 0),
                                       stop=(k == FC - 1))
                    mm.then_inc(s_ffn, 1)
                s(4)
                if there(b, BLOCKS):
                    wait(pe, s_on, b + 1)
                    wait(pe, s_mt, seen(b + 3))
                    for k in range(FC):
                        mm = pe.transpose(trbank[:, k * P:(k + 1) * P], on[:, k * P:(k + 1) * P], idf[:])
                    mm.then_inc(s_ntp, 1)
                st(2)
                s(5)
                st(3)
                s(6)
                if there(b, BLOCKS):
                    wait(pe, s_onT, b + 1)
                    wait(pe, s_ob, b)
                    for k in range(FC):
                        mm = pe.matmul(dbank[:, 0:WIDTH], onT[:, k], wf[:, k], start=(k == 0),
                                       stop=(k == FC - 1))
                    mm.then_inc(s_wf, 1)
                s(7)
                st(4)

            between(p1, p2, hand_over)
            p2_loop(pe, p2)

        @block.scalar
        def _(act):
            def p1(s, par):
                tr, pj = s + 1, s
                def q1(h):
                    if there(pj, TILES):
                        wait(act, s_q, FC * pj + h + 1)
                        act.copy(qp[:, par, 0, h], qbank[:, h]).then_inc(s_q1, 1)

                if there(pj, TILES):
                    wait(act, s_kv, pj + 1)
                    wait(act, s_vt, pj)
                    wait(act, s_kr, pj)
                    act.copy(kvS[:], bank[2][:, 0:P]).then_inc(s_kvs, 1)
                    wait(act, s_stq[par], S_DMAS * 16 * (pj // 2))
                q1(0)
                if there(pj, TILES):
                    wait(act, s_kvs, pj + 1)
                    act.copy(kp[:, par, 2], kvS[:]).then_inc(s_k1, 1)
                if there(tr, TILES):
                    wait(act, s_q, FC * (tr - 1))
                    for c in range(FC):
                        wait(act, s_tr1, tr * FC + c + 1)
                        act.copy(xnT[:, 1 - par, c], bank[c][:, :]).then_inc(s_xnT, 1)
                if there(pj, TILES):
                    wait(act, s_kr, pj + 1)
                    act.copy(kp[:, par, 1], kr[:]).then_inc(s_k2, 1)
                q1(1)
                if there(pj, TILES):
                    for h in range(FC):
                        wait(act, s_qr, FC * pj + h + 1)
                        act.copy(qp[:, par, 1, h], qr[:, h]).then_inc(s_q2, 1)

            def setup(k):
                if k == 0:
                    act.wait_ge(s_low, 1)
                    act.copy(low1[:], bank[4][0:RANK, 0:WIDTH]).then_inc(s_lowc, 1)
                elif k == 1:
                    act.wait_ge(s_low, 2)
                    act.copy(low2[:], bank[4][0:UDIM, 0:WIDTH]).then_inc(s_lowc, 1)

            p1_loop(act, p1, setup)

            def exps(n, u, j):
                par = u % 2
                wait(act, s_stp, STU * n + j + 1)
                if j == 0:
                    wait(act, s_pv, n - 1)
                dst = pm[:, par, j] if j < GROUPS else pr[:, par]
                act.activation(dst, tbank[(STU * u + j) % 2][:, :], ACT.Exp, scale=SCALE).then_inc(s_ex, 1)

            def p2(n, u):
                m, c, b, e = n - 1, n - 2, n - 3, n - 4
                uc = (u - 2) % 4

                def ex(*units):
                    if there(c, BLOCKS):
                        for j in units:
                            exps(c, uc, j)

                def q_groups(*groups):
                    a, v = n + 1, (u + 1) % 4
                    if there(a, BLOCKS):
                        for g in groups:
                            wait(act, s_qin[v // 2], 16 * Q_DMAS * (a // 4 + 1))
                            wait(act, s_stp, STU * (a - 3))
                            at = (v % 2) * P + g * GQ
                            act.copy(qs[0:KROWS, v, g], qin[:, v // 2, :, at:at + GQ]).then_inc(s_qs, 1)

                q_groups(0)
                q_groups(1)
                if there(m, BLOCKS):
                    wait(act, s_mtp, m + 1)
                    wait(act, s_m[(u - 3) % 4], 16 * ((m - 2) // 4 + 1))
                    act.copy(mt[:, (u - 1) % 2], trbank[0:PARTS * 16, 0:P // 2].bitcast(BF16)).then_inc(s_mt, 1)
                if there(e, BLOCKS):
                    wait(act, s_xtp, e + 1)
                    wait(act, s_ffn, e)
                    act.copy(x2nT[:].rearrange("p c t -> p (c t)"), xtbank[:, 0:WIDTH]).then_inc(s_x2nT, 1)
                ex(0)
                q_groups(2)
                ex(1)
                q_groups(3)
                if there(b, BLOCKS):
                    wait(act, s_ntp, b + 1)
                    wait(act, s_wf, b)
                    act.copy(onT[:].rearrange("p c t -> p (c t)"), trbank[:, 0:WIDTH]).then_inc(s_onT, 1)
                ex(2)
                ex(3)
                ex(4)

            def hand_over(n):
                if n == 0:
                    act.wait_ge(s_qs, GROUPS)

            between(p1, p2, hand_over)
            p2_loop(act, p2)

        @block.vector
        def _(dve):
            dve.memset(zero[:], 0.0).then_inc(s_zero, 1)
            dve.memset(neghalf[:], -0.5)
            dve.memset(bdmask[:], 0.0)
            dve.memset(vn[:], 0.0)
            dve.memset(mp[:], 0.0).then_inc(s_set, 1)
            dve.wait_ge(s_set, 1)
            dve.memset(vn[:, :, :, HD:HD + 1], 1.0)
            for g in range(GROUPS):
                last = dve.memset(bdmask[g * GQ:(g + 1) * GQ, g], 1.0)
            last.then_inc(s_set, 1)
            def p1(s, par):
                ln, pj, vt = s + 2, s, s - 1
                if there(ln, TILES):
                    wait(dve, s_x1[par], 16 * (ln // 2 + 1))
                    wait(dve, s_mv1, TJ * ln)
                    for j in range(TJ):
                        dve.bn_stats(st1[:, j], xt[:, par, j]).then_inc(s_st1, 1)
                    wait(dve, s_st1, TJ * (ln + 1))
                    wait(dve, s_xn, ln)
                    dve.memset(tick[:], 0.0)
                    for j in range(TJ):
                        dve.bn_aggr(mv1[:, j], st1[:, j]).then_inc(s_mv1, 1)
                    wait(dve, s_mv1, TJ * (ln + 1))
                    wait(dve, s_rs1, ln)
                    dve.tensor_scalar(ve1[:], mv1[:, :, 1], EPS, None, ALU.add).then_inc(s_ve1, 1)
                def remainder(h):
                    if there(pj, TILES):
                        wait(dve, s_q1, FC * pj + h + 1)
                        wait(dve, s_q3, FC * (pj - 1) + h + 1)
                        dve.tensor_tensor(qr[:, h], qbank[:, h], qp[:, par, 0, h], ALU.subtract
                                          ).then_inc(s_qr, 1)

                remainder(0)
                if there(vt, TILES):
                    wait(dve, s_vt, vt + 1)
                    wait(dve, s_stv[1 - par], 16 * (vt // 2))
                    dve.tensor_copy(vn[:, 1 - par, :, 0:HD],
                                    bank[3][:, 0:P].rearrange("p (j c) -> p j c", c=KV)[:, :, HD:KV]
                                    ).then_inc(s_vn, 1)
                if there(ln, TILES):
                    wait(dve, s_rs1, ln + 1)
                    wait(dve, s_tr1, FC * (ln - 1))
                    for j in range(TJ):
                        last = dve.tensor_scalar(xn[:, par, j], xt[:, par, j], mv1[:, j, 0:1], rs1[:, j:j + 1],
                                                 ALU.subtract, ALU.mult)
                    last.then_inc(s_xn, 1)
                remainder(1)

            def setup(k):
                if k == 0:
                    dve.wait_ge(s_const, 16 * (len(consts) - EARLY))
                elif k == 2:
                    dve.wait_ge(s_low, 3)
                    dve.tensor_tensor(weff[:].rearrange("p c n -> p (c n)"), bank[4][:, :],
                                      wffn[:].rearrange("p c n -> p (c n)"), ALU.add).then_inc(s_weff, 1)

            p1_loop(dve, p1, setup)

            def p2(n, u):
                m, b, e = n - 1, n - 3, n - 4
                par = u % 2

                def mx_(*units):
                    if there(n, BLOCKS):
                        for j in units:
                            wait(dve, s_sc, UNITS * n + j + 1)
                            dve.tensor_reduce(mx[:, par, 2 * j:2 * j + 2],
                                              sbank[j % 2][:, 0:2 * GWIN].rearrange("p (k c) -> p k c", k=2),
                                              AX.X, ALU.max).then_inc(s_mx, 1)

                m_ = mx[:, (u - 1) % 2]
                if there(e, BLOCKS):
                    wait(dve, s_st2, e + 1)
                    dve.memset(tick[:], 0.0)
                    dve.bn_aggr(mv2[:], st2[:]).then_inc(s_mv2, 1)
                if there(m, BLOCKS):
                    wait(dve, s_mx, UNITS * (m + 1))
                    wait(dve, s_mtp, m)
                    dve.tensor_copy(mp[:, 0], m_).then_inc(s_mp1, 1)
                if there(e, BLOCKS):
                    wait(dve, s_mv2, e + 1)
                    dve.tensor_scalar(ve2[:], mv2[:, 1:2], EPS, None, ALU.add).then_inc(s_ve2, 1)
                if there(m, BLOCKS):
                    wait(dve, s_mp1, m + 1)
                    dve.tensor_tensor(mr[:, 0], m_, mp[:, 0], ALU.subtract).then_inc(s_mr1, 1)
                    wait(dve, s_mr1, m + 1)
                    dve.tensor_copy(mp[:, 1], mr[:, 0]).then_inc(s_mp2, 1)
                mx_(0)
                if there(m, BLOCKS):
                    wait(dve, s_mp2, m + 1)
                    dve.tensor_tensor(mp[:, 2], mr[:, 0], mp[:, 1], ALU.subtract).then_inc(s_mp, 1)
                if there(e, BLOCKS):
                    wait(dve, s_rs2, e + 1)
                    wait(dve, s_xtp, e)
                    dve.tensor_scalar(x2n[:], x2[:], mv2[:, 0:1], rs2[:], ALU.subtract, ALU.mult
                                      ).then_inc(s_x2n, 1)
                mx_(1)
                if there(b, BLOCKS):
                    wait(dve, s_pv, b + 1)
                    wait(dve, s_on, b)
                    dve.transpose(ot[:].rearrange("p h c -> p (h c)"), pvbank[:, :]).then_inc(s_ot, 1)
                mx_(2)
                if there(b, BLOCKS):
                    wait(dve, s_ot, b + 1)
                    dve.reciprocal(rden[:], ot[:, :, HD]).then_inc(s_rd, 1)
                    wait(dve, s_rd, b + 1)
                    wait(dve, s_ntp, b)
                    dve.tensor_tensor(on[:].rearrange("p (h d) -> p h d", d=HD), ot[:, :, 0:HD],
                                      rden[:].unsqueeze(2).to_broadcast([P, HEADS, HD]), ALU.mult
                                      ).then_inc(s_on, 1)
                mx_(3)
                mx_(4)
                if there(e, BLOCKS):
                    wait(dve, s_ffn, e + 1)
                    wait(dve, s_x2b, e + 1)
                    wait(dve, s_out[u % 4 // 2], 16 * (e // 4))
                    dve.tensor_tensor(ob[:, u], dbank[:, 0:WIDTH], x2b[:], ALU.add).then_inc(s_ob, 1)
                mx_(5)
                mx_(6)
                if there(b, BLOCKS):
                    wait(dve, s_wf, b + 1)
                    wait(dve, s_xb, b + 1)
                    wait(dve, s_x2b, b)
                    dve.tensor_tensor(x2[:], dbank[:, 0:WIDTH], xr[:, (u - 3) % 4], ALU.add).then_inc(s_x2, 1)
                    wait(dve, s_x2, b + 1)
                    dve.bn_stats(st2[:], x2[:]).then_inc(s_st2, 1)
                mx_(7)

            def hand_over(n):
                if n == -1:
                    dve.wait_ge(s_qin[0], 16 * Q_DMAS)
                    dve.tensor_copy(qs[0:KROWS, 0], qin[:, 0, :, 0:P].rearrange("p h (g q) -> p g h q", q=GQ)
                                    ).then_inc(s_qs, GROUPS)

            between(p1, p2, hand_over)
            p2_loop(dve, p2)

        @block.gpsimd
        def _(pool):
            pool.wait_ge(s_set, 2)

            def p1(s, par):
                ln, pj = s + 2, s
                if there(ln, TILES):
                    wait(pool, s_ve1, ln + 1)
                    wait(pool, s_xn, ln)
                    pool.tensor_tensor(rs1[:], ve1[:], neghalf[:], ALU.pow).then_inc(s_rs1, 1)
                if there(pj, TILES):
                    wait(pool, s_k1, pj + 1)
                    wait(pool, s_k3, pj)
                    pool.tensor_tensor(kr[:], kvS[:], kp[:, par, 2], ALU.subtract).then_inc(s_kr, 1)
                    wait(pool, s_k2, pj + 1)
                    pool.tensor_tensor(kp[:, par, 0], kr[:], kp[:, par, 1], ALU.subtract).then_inc(s_k3, 1)
                    for h in range(FC):
                        wait(pool, s_q2, FC * pj + h + 1)
                        pool.tensor_tensor(qp[:, par, 2, h], qr[:, h], qp[:, par, 1, h], ALU.subtract
                                           ).then_inc(s_q3, 1)

            def setup(k):
                if k == 0:
                    pool.wait_ge(s_const, 16 * (len(consts) - EARLY))

            p1_loop(pool, p1, setup)

            def p2(n, u):
                c, e = n - 2, n - 4
                uc = (u - 2) % 4

                def select(g):
                    wait(pool, s_ex, STU * c + g + 1)
                    pool.tensor_tensor(ptick[:, g:g + 1], neghalf[0:1, 0:1], neghalf[0:1, 0:1], ALU.add)
                    v = pm[0:GQ, uc % 2, g].rearrange("p (h q) -> p h q", h=HEADS)
                    pool.affine_select(out=v, in_=v, compare_op=ALU.is_ge, fill=0.0, base=0,
                                       pattern=[[0, HEADS], [-1, GQ]], channel_multiplier=1).then_inc(s_sel, 1)

                if there(e, BLOCKS):
                    wait(pool, s_ve2, e + 1)
                    wait(pool, s_x2n, e)
                    pool.tensor_tensor(rs2[:], ve2[:], neghalf[:, 0:1], ALU.pow).then_inc(s_rs2, 1)
                if there(c, BLOCKS):
                    wait(pool, s_xin[uc // 2], 16 * (c // 4 + 1))
                    pool.tensor_tensor(xr[:, uc], xr[:, uc], bf_bc[:], ALU.add).then_inc(s_xb, 1)
                    wait(pool, s_v[uc], 16 * (c // 4 + 1))
                    wait(pool, s_pv, c - 1)
                    pool.tensor_tensor(vbd[:, uc % 2], vm[:, uc, GROUPS].unsqueeze(1).to_broadcast([P, GROUPS, VW]),
                                       bdmask[:], ALU.mult).then_inc(s_vbd, 1)
                if there(e, BLOCKS):
                    wait(pool, s_x2, e + 1)
                    wait(pool, s_ob, e)
                    pool.tensor_tensor(x2b[:], x2[:], b_bc[:], ALU.add).then_inc(s_x2b, 1)
                if there(c, BLOCKS):
                    select(0)
                    select(1)
                    select(2)
                    select(3)

            between(p1, p2)
            p2_loop(pool, p2)


def kernel(L0_attn_x, L0_attn_Wq, L0_attn_Wk, L0_attn_Wv, L0_attn_Wf, L0_attn_bf, L0_ffn_W, L0_ffn_b,
           L0_ffn_lora_down, L0_ffn_lora_up, L0_ffn_down_aux, L0_ffn_up_aux):
    import ml_dtypes
    import numpy as np
    import concourse.bacc as bacc
    from concourse.bass_utils import run_bass_kernel_spmd

    bf = ml_dtypes.bfloat16
    f = np.float32
    wkv = np.concatenate([np.asarray(L0_attn_Wk), np.asarray(L0_attn_Wv)], axis=0).T
    edge = np.zeros((1 + PARTS, BATCH, LP), f)
    edge[0, :, 0:WINDOW] = NEG
    edge[0, :, WINDOW + SEQ:] = NEG
    edge[1:] = -1.0
    i = np.arange(GQ)
    onehot = np.tile(np.eye(GQ, dtype=f), (1, P // GQ))
    corner = np.zeros((GQ, 2, 2, GQ), f)
    corner[:, :, 0] = np.where(i[None, :] < i[:, None], NEG, 0.0)[:, None, :]
    corner[:, :, 1] = np.where(i[None, :] > i[:, None], NEG, 0.0)[:, None, :]
    rem = np.tile(np.where(i[None, :] > i[:, None], NEG, 0.0), (1, GROUPS))
    data = {
        "x": np.asarray(L0_attn_x).reshape(TOKENS, WIDTH),
        "wq_t": np.asarray(L0_attn_Wq).T, "wkv_t": wkv, "wf_t": np.asarray(L0_attn_Wf).T,
        "bf_rows": np.broadcast_to(np.asarray(L0_attn_bf), (P, WIDTH)),
        "wffn_t": np.asarray(L0_ffn_W).T, "b_rows": np.broadcast_to(np.asarray(L0_ffn_b), (P, WIDTH)),
        "down_t": np.asarray(L0_ffn_lora_down).T, "up_t": np.asarray(L0_ffn_lora_up).T,
        "down_aux": np.asarray(L0_ffn_down_aux), "up_aux_t": np.asarray(L0_ffn_up_aux).T,
        "edge_rows": edge.reshape(1 + PARTS, BATCH * LP).astype(bf),
        "onehot": onehot.astype(bf), "corners": corner.astype(bf), "rem_mask": rem.astype(bf),
        "onehot_cols": np.tile(np.eye(GQ, dtype=f), (1, HEADS)).astype(bf),
        "ident": np.eye(P, dtype=f), "ident_b": np.eye(P, dtype=f).astype(bf),
        "ones_row": np.ones((1, RING * HEADS * P), bf),
    }
    nc = bacc.Bacc("TRN2", target_bir_lowering=False, num_devices=1)
    arrays, args = {}, []
    for name, a in data.items():
        arrays[f"in_{name}"] = a = np.ascontiguousarray(a)
        args.append(nc.dram_tensor(f"in_{name}", a.shape, mybir.dt.from_np(a.dtype), kind="ExternalInput").ap())
    args.append(nc.dram_tensor("out_y", (TOKENS, WIDTH), F32, kind="ExternalOutput").ap())
    build(nc, *args)
    r = run_bass_kernel_spmd(nc, [arrays], core_ids=[0])
    return r.results[0]["out_y"].reshape(BATCH, SEQ, WIDTH)
```
